# Optimizing a Trainium2 kernel written in Bass

```python
import numpy as np
import jax
import jax.numpy as jnp

def _softmax(x, axis=-1):
    return jax.nn.softmax(x, axis=axis)

def _gelu(x):
    return jax.nn.gelu(x, approximate=True)

def _silu(x):
    return jax.nn.silu(x)

def _sigmoid(x):
    return jax.nn.sigmoid(x)

def _layernorm(x, axis=-1, eps=1e-05):
    m = jnp.mean(x, axis=axis, keepdims=True)
    v = jnp.var(x, axis=axis, keepdims=True)
    return (x - m) / jnp.sqrt(v + eps)

def _scatter_add(tgt, idx, src, axis=0):
    return tgt.at[idx].add(src)

def _segment_sum(src, seg, n):
    return jax.ops.segment_sum(src, seg, n)
kernel_name = 'mk_xattn_ffn_d1_seqx_r8_b22984'

def setup_inputs(seed: int=0):
    np.random.seed(seed)
    _w = jnp.asarray

    def _rec_inputs():
        import jax
        import jax.numpy as jnp
        _rk = jax.random.key(seed)
        x = 7.22e-05 + 1 * jax.random.normal(jax.random.fold_in(_rk, 1), (1, 1024, 128), jnp.float32)
        _lenS = 1024 - jax.random.randint(jax.random.fold_in(_rk, 7), (1,), 0, max(1, 1024 // 4) + 1, jnp.int32)
        _lenS2 = 6404 - jax.random.randint(jax.random.fold_in(_rk, 8), (1,), 0, max(1, 6404 // 4) + 1, jnp.int32)
        _ctx_1024P = jax.random.normal(jax.random.fold_in(_rk, 11), (1, 16, 128), jnp.float32)
        _ctx_1024c = jax.random.dirichlet(jax.random.fold_in(_rk, 511), 0.3 * jnp.ones((16,), jnp.float32), (1, 6404))
        _ctx_1024t = jnp.einsum('bsk,bkd->bsd', _ctx_1024c, _ctx_1024P)
        _ctx_1024t = _ctx_1024t * jax.lax.rsqrt(jnp.mean(jnp.square(_ctx_1024t)) + 1e-12) * 0.953939
        ctx_1024 = 2.81802e-05 + 1.00001 * (_ctx_1024t + 0.3 * jax.random.normal(jax.random.fold_in(_rk, 611), (1, 6404, 128), jnp.float32))
        _validS = jnp.arange(1024)[None, :] < _lenS[:, None]
        _validS2 = jnp.arange(6404)[None, :] < _lenS2[:, None]
        _causal = jnp.tril(jnp.ones((1024, 1024), dtype=bool))
        mask_BxS2_bk0 = jnp.logical_not(jnp.broadcast_to(_validS2[:, :], (1, 6404)))
        return (x, ctx_1024, mask_BxS2_bk0)
    x, ctx_1024, mask_BxS2_bk0 = _rec_inputs()

    def _L0_xattn_setup():
        import jax, jax.numpy as jnp
        import numpy as np
        B, LQ, LKV = (8, 128, 256)
        QDIM, KDIM, HID = (128, 128, 128)
        key = jax.random.key(seed)
        ks = jax.random.split(key, 12)
        s = lambda d: 1.0 / np.sqrt(d)
        return {'query': jax.random.normal(ks[0], (B, LQ, QDIM), jnp.float32), 'key_value': jax.random.normal(ks[1], (B, LKV, KDIM), jnp.float32), 'key_mask': jax.random.randint(ks[2], (B, LKV), 0, 2).astype(bool), 'Wq': jax.random.uniform(ks[3], (QDIM, HID), jnp.float32, -s(QDIM), s(QDIM)), 'bq': jax.random.uniform(ks[4], (HID,), jnp.float32, -s(QDIM), s(QDIM)), 'Wk': jax.random.uniform(ks[5], (KDIM, HID), jnp.float32, -s(KDIM), s(KDIM)), 'bk': jax.random.uniform(ks[6], (HID,), jnp.float32, -s(KDIM), s(KDIM)), 'Wv': jax.random.uniform(ks[7], (KDIM, HID), jnp.float32, -s(KDIM), s(KDIM)), 'bv': jax.random.uniform(ks[8], (HID,), jnp.float32, -s(KDIM), s(KDIM)), 'Wo': jax.random.uniform(ks[9], (HID, QDIM), jnp.float32, -s(HID), s(HID)), 'bo': jax.random.uniform(ks[10], (QDIM,), jnp.float32, -s(HID), s(HID))}
    _L0_xattn_all = _L0_xattn_setup()
    _L0_xattn_in = {k: v for k, v in _L0_xattn_all.items() if k in ('Wq', 'bq', 'Wk', 'bk', 'Wv', 'bv', 'Wo', 'bo')}
    del _L0_xattn_all

    def _L0_ffn_setup():
        import jax, jax.numpy as jnp
        import numpy as np
        N_EXPERTS = 8
        N_GROUP = 4
        TOPK_GROUP = 2
        TOP_K = 2
        HIDDEN = 128
        INTER = 256
        B, S = (1, 128)

        def _grouped_topk(scores):
            T, E = scores.shape
            per_group = E // N_GROUP
            group_scores = scores.reshape(T, N_GROUP, per_group).max(-1)
            _, gidx = jax.lax.top_k(group_scores, TOPK_GROUP)
            gmask = jnp.zeros((T, N_GROUP), scores.dtype).at[jnp.arange(T)[:, None], gidx].set(1.0)
            smask = jnp.repeat(gmask, per_group, axis=1)
            masked = jnp.where(smask > 0, scores, 0.0)
            topk_w, topk_ids = jax.lax.top_k(masked, TOP_K)
            topk_w = topk_w / topk_w.sum(-1, keepdims=True)
            return (topk_ids, topk_w)
        key = jax.random.key(seed)
        k1, k2, k3, k4 = jax.random.split(key, 4)
        return {'hidden_states': jax.random.normal(k1, (B, S, HIDDEN), jnp.float32), 'gate_w': jax.random.normal(k2, (N_EXPERTS, HIDDEN), jnp.float32) * 0.02, 'w13_weight': jax.random.normal(k3, (N_EXPERTS, 2 * INTER, HIDDEN), jnp.float32) * 0.02, 'w2_weight': jax.random.normal(k4, (N_EXPERTS, HIDDEN, INTER), jnp.float32) * 0.02}
    _L0_ffn_all = _L0_ffn_setup()
    _L0_ffn_in = {k: v for k, v in _L0_ffn_all.items() if k in ('gate_w', 'w13_weight', 'w2_weight')}
    del _L0_ffn_all
    return {'x': x, 'ctx_1024': ctx_1024, 'mask_BxS2_bk0': mask_BxS2_bk0, 'L0_xattn_Wq': _L0_xattn_in['Wq'], 'L0_xattn_bq': _L0_xattn_in['bq'], 'L0_xattn_Wk': _L0_xattn_in['Wk'], 'L0_xattn_bk': _L0_xattn_in['bk'], 'L0_xattn_Wv': _L0_xattn_in['Wv'], 'L0_xattn_bv': _L0_xattn_in['bv'], 'L0_xattn_Wo': _L0_xattn_in['Wo'], 'L0_xattn_bo': _L0_xattn_in['bo'], 'L0_ffn_gate_w': _L0_ffn_in['gate_w'], 'L0_ffn_w13_weight': _L0_ffn_in['w13_weight'], 'L0_ffn_w2_weight': _L0_ffn_in['w2_weight']}

def reference(x, ctx_1024, mask_BxS2_bk0, L0_xattn_Wq, L0_xattn_bq, L0_xattn_Wk, L0_xattn_bk, L0_xattn_Wv, L0_xattn_bv, L0_xattn_Wo, L0_xattn_bo, L0_ffn_gate_w, L0_ffn_w13_weight, L0_ffn_w2_weight):
    import jax
    import jax.numpy as jnp

    def _L0_xattn_ref(query, key_value, key_mask, Wq, bq, Wk, bk, Wv, bv, Wo, bo):
        import jax, jax.numpy as jnp
        import numpy as np
        B, LQ, LKV = (8, 128, 256)
        QDIM, KDIM, HID = (128, 128, 128)
        Q = query @ Wq + bq
        K = key_value @ Wk + bk
        V = key_value @ Wv + bv
        hid = Q.shape[-1]
        scores = jnp.einsum('bqh,bkh->bqk', Q, K) / jnp.sqrt(jnp.float32(hid))
        scores = jnp.where(key_mask[:, None, :], scores, jnp.float32(-1000000000.0))
        attn = jax.nn.softmax(scores, axis=-1)
        context = jnp.einsum('bqk,bkh->bqh', attn, V)
        return context @ Wo + bo

    def _L0_ffn_ref(hidden_states, gate_w, w13_weight, w2_weight):
        import jax, jax.numpy as jnp
        import numpy as np
        N_EXPERTS = 8
        N_GROUP = 4
        TOPK_GROUP = 2
        TOP_K = 2
        HIDDEN = 128
        INTER = 256
        B, S = (1, 128)

        def _grouped_topk(scores):
            T, E = scores.shape
            per_group = E // N_GROUP
            group_scores = scores.reshape(T, N_GROUP, per_group).max(-1)
            _, gidx = jax.lax.top_k(group_scores, TOPK_GROUP)
            gmask = jnp.zeros((T, N_GROUP), scores.dtype).at[jnp.arange(T)[:, None], gidx].set(1.0)
            smask = jnp.repeat(gmask, per_group, axis=1)
            masked = jnp.where(smask > 0, scores, 0.0)
            topk_w, topk_ids = jax.lax.top_k(masked, TOP_K)
            topk_w = topk_w / topk_w.sum(-1, keepdims=True)
            return (topk_ids, topk_w)
        Bm, Sm, H = hidden_states.shape
        x = hidden_states.reshape(-1, H)
        T = x.shape[0]
        scores = jax.nn.softmax(x @ gate_w.T, axis=-1)
        topk_ids, topk_w = _grouped_topk(scores)
        combine = jnp.zeros((T, N_EXPERTS), x.dtype).at[jnp.arange(T)[:, None], topk_ids].add(topk_w)
        gu = jnp.einsum('th,eih->tei', x, w13_weight)
        gate, up = (gu[..., :INTER], gu[..., INTER:])
        act = jax.nn.silu(gate) * up
        act = act * combine[:, :, None]
        out = jnp.einsum('tei,ehi->th', act, w2_weight)
        return out.reshape(Bm, Sm, H)
    x = x + _L0_xattn_ref(_layernorm(x, axis=-1), ctx_1024, mask_BxS2_bk0, L0_xattn_Wq, L0_xattn_bq, L0_xattn_Wk, L0_xattn_bk, L0_xattn_Wv, L0_xattn_bv, L0_xattn_Wo, L0_xattn_bo)
    x = x + _L0_ffn_ref(_layernorm(x, axis=-1), L0_ffn_gate_w, L0_ffn_w13_weight, L0_ffn_w2_weight)
    return x

_drawn_inputs = setup_inputs


def setup_inputs(seed=0):
    import zlib

    import numpy as np

    out = dict(_drawn_inputs(seed))
    spreads = {}
    factors = {'L0_xattn_bq': 8.0,
     'L0_xattn_Wk': 2.681,
     'L0_xattn_bk': 8.0,
     'L0_ffn_gate_w': 8.0,
     'L0_ffn_w13_weight': 8.0,
     'L0_ffn_w2_weight': 8.0}
    for name, (base, spread) in spreads.items():
        noise = np.random.default_rng([zlib.crc32(name.encode()), seed]).standard_normal(out[name].shape)
        drawn = base * np.exp(spread * noise) if base else spread * noise
        out[name] = jnp.asarray(drawn.astype(out[name].dtype))
    for name, factor in factors.items():
        out[name] = (out[name] * factor).astype(out[name].dtype)
    return out
```

```python
from contextlib import ExitStack

import concourse.bass as bass
from concourse import mybir

F32 = mybir.dt.float32
F32R = mybir.dt.float32r
BF16 = mybir.dt.bfloat16
I32 = mybir.dt.int32
ALU = mybir.AluOpType
ACT = mybir.ActivationFunctionType
X = mybir.AxisListType.X

P = 128
HALF = 512
CHUNK = 2 * P
MASKED = -1.0e9
PADDED = -3.0e9
LOWEST = -3.0e38
EPS = 1e-5
BLOCK = 7
SCORE_BANK = (4, 5, 6, 5)
KEY_BANK = 7
SCORE_WAIT = (1, 4, 3, 6)


class Chain:

    def __init__(self, engine, sem):
        self.engine, self.sem, self.value = engine, sem, 0

    def link(self, instruction):
        instruction.then_inc(self.sem, 1)
        self.value += 1

    def settle(self):
        self.engine.wait_ge(self.sem, self.value)

    def step(self, instruction):
        self.link(instruction)
        self.settle()


def xattn_ffn(nc, keys, x, mask, ctx_t, ctx_n, Wq, bq, Wk, bk, Wv, bv, Wo, bo, gate_t, w13_t, w2_t, out_t):
    TOKENS = x.shape[0]
    NT = TOKENS // P
    HT = HALF // P
    KT = 4 * mask.shape[1]
    NC = KT // 2
    PAD = ctx_t.shape[1] - keys
    E = w13_t.shape[1]
    SCALE = float(P) ** -0.5
    EG = 2
    G = E // EG
    TOP = 2
    assert TOKENS == 2 * HALF and ctx_t.shape[1] == KT * P and PAD >= 0

    with ExitStack() as ctx:
        def sb(name, shape, dt=F32):
            return ctx.enter_context(nc.sbuf_tensor(name, shape, dt))

        def sem(name):
            return ctx.enter_context(nc.semaphore(name))

        bank = [ctx.enter_context(nc.psum_tensor(f"bank{i}", [P, HALF], F32)) for i in range(8)]

        ident = sb("ident", [P, P])
        ones_f = sb("ones_f", [P, P])
        ones_r = sb("ones_r", [P, P], F32R)
        zeros_b = sb("zeros_b", [P, HALF], BF16)
        neg_half = sb("neg_half", [P, NT])
        chunk_no = sb("chunk_no", [1, 2, NC])
        earlier = sb("earlier", [P, E, E])
        row_mask = sb("row_mask", [2 * E, E])

        x_n = sb("x_n", [P, NT, P])
        bo_row = sb("bo_row", [P, P])
        mask_u = sb("mask_u", [P, KT], mybir.dt.uint8)
        keys_t = sb("keys_t", [P, KT * P])
        keys_n = sb("keys_n", [P, KT, P])
        wq, wk, wv, wo = (sb(n, [P, P]) for n in ("wq", "wk", "wv", "wo"))
        bq_c, bk_c, bv_c = (sb(n, [P, 1]) for n in ("bq_c", "bk_c", "bv_c"))
        gate = sb("gate", [P, E])
        w_f = sb("w_f", [P, E, 6 * P])

        def parts(name, shape):
            return sb(name + "_hi", shape, F32R), sb(name + "_lo", shape, F32R)

        wq_p, wv_p, wo_p = parts("wq_p", [P, P]), parts("wv_p", [P, P]), parts("wo_p", [P, P])
        gate_p = parts("gate_p", [P, E])
        xt_p = parts("xt_p", [P, TOKENS])
        q_p = parts("q_p", [P, TOKENS])
        k_p = parts("k_p", [P, 2, P])
        v_p = parts("v_p", [P, 2, P])
        p_p = parts("p_p", [P, 4, HALF])
        w_p = [parts(f"w_p{i}", [P, 6 * P]) for i in range(2)]

        stats = sb("stats", [P, NT, 6])
        mv = sb("mv", [P, NT, 2])
        var = sb("var", [P, NT])
        rstd = sb("rstd", [P, NT])
        xn = sb("xn", [P, NT, P])
        mask_f = sb("mask_f", [P, KT])
        key_scale = sb("key_scale", [P, KT])
        key_bias0 = sb("key_bias0", [P, KT])
        key_bias = sb("key_bias", [P, KT])
        count = sb("count", [1, NC])
        marked = sb("marked", [1, 2, NC])
        edge = sb("edge", [1, 2])
        none = sb("none", [1, 2])
        edge2 = sb("edge2", [1, 2])
        span = sb("span", [1, 4])
        over = sb("over", [1, 3])
        bounds = sb("bounds", [1, 4], I32)
        scores = sb("scores", [P, 2 * BLOCK, TOKENS])
        run_max = sb("run_max", [P, TOKENS])
        max_col = sb("max_col", [P, NT])
        max_mat = xn
        max_b = sb("max_b", [P, TOKENS])
        alpha = xn[:, :, :].rearrange("p a b -> p (a b)")
        late_at = [0]

        def late(*shape, rows=P):
            size = 1
            for n in shape:
                size *= n
            at = late_at[0]
            late_at[0] += size
            assert late_at[0] <= 2 * BLOCK * TOKENS
            flat = scores[0:rows, :, :].rearrange("p a b -> p (a b)")[:, at:at + size]
            if len(shape) == 1:
                return flat
            names = "abc"[:len(shape)]
            return flat.rearrange(f"p ({' '.join(names)}) -> p {' '.join(names)}",
                                  **dict(zip(names[1:], shape[1:])))

        rsum = late(TOKENS)
        o_n = late(TOKENS)
        x1 = late(NT, P)
        x1_t = late(TOKENS)
        out_s = late(TOKENS)
        r8 = [late(NT, E) for i in range(8)]
        r1 = [late(NT) for i in range(3)]
        g4 = [late(NT, G) for i in range(3)]
        pair = [late(NT, E, E) for i in range(2)]
        comb = late(NT, 2 * E)
        comb_t = late(TOKENS, rows=2 * E)
        comb_e = [q[0:2 * E, :] for q in q_p]
        silu = late(2, HALF)
        silc = late(2, HALF)
        inner = late(4, HALF)

        (mask_in, x_in, wq_in, wk_in, wv_in, col_in, gate_in, w_in, bo_in, keys_t_in, keys_n_in, out_sent,
         consts, mask_conv, key_cols, count_ps, bounds_ok, pool_w, pool_k, norm_var, norm_rstd, norm_x, tr_ps,
         xt_hi, xt_lo, q_ps, q_hi, q_lo, acc_zero, key_ps, k_hi, k_lo, score_ps, score_kept, max_run,
         max_tr, max_cols, max_ps, max_ok, old_diff, alpha_ok, shifted, shifted_pool, prob, prob_hi, prob_lo,
         prob_lo_pool, v_ok, pv, attn_end, o_norm, o_hi, o_lo, val_ps, val_hi, val_lo, attn_ps, x1_ok, x1_tr_ps,
         x1_t_ok, logit_ps, logit_exp, logit_sub, comb_ok, comb_ps, comb_t_ok, comb_e_ok, comb_b, w_hi, w_lo, gate_ps, up_ps,
         silu_ok, silc_ok, inner_ok, inner_hi, inner_lo, down, y_end, out_ok, dve_chain, xb_ok) = (
            sem(n) for n in (
                "mask_in x_in wq_in wk_in wv_in col_in gate_in w_in bo_in keys_t_in keys_n_in out_sent "
                "consts mask_conv key_cols count_ps bounds_ok pool_w pool_k norm_var norm_rstd norm_x tr_ps "
                "xt_hi xt_lo q_ps q_hi q_lo acc_zero key_ps k_hi k_lo score_ps score_kept max_run "
                "max_tr max_cols max_ps max_ok old_diff alpha_ok shifted shifted_pool prob prob_hi prob_lo "
                "prob_lo_pool v_ok pv attn_end o_norm o_hi o_lo val_ps val_hi val_lo attn_ps x1_ok x1_tr_ps "
                "x1_t_ok logit_ps logit_exp logit_sub comb_ok comb_ps comb_t_ok comb_e_ok comb_b w_hi w_lo gate_ps up_ps "
                "silu_ok silc_ok inner_ok inner_hi inner_lo down y_end out_ok dve_chain xb_ok").split())

        def half(t, h):
            return t[:, h * HALF:(h + 1) * HALF]

        def tile(t, i):
            return t[:, i * P:(i + 1) * P]

        def f(ap):
            return ap.bitcast(F32)

        def load_bounds(eng):
            eng.wait_ge(bounds_ok, 1)
            first = eng.value_load(bounds[0:1, 0:1], min_val=0, max_val=NC - 1)
            end = eng.value_load(bounds[0:1, 1:2], min_val=1, max_val=NC)
            blocks = eng.value_load(bounds[0:1, 2:3], min_val=1, max_val=-(-NC // BLOCK))
            chunks = eng.value_load(bounds[0:1, 3:4], min_val=1, max_val=NC)
            return first, end, blocks, chunks

        def least(eng, a, b, low, high):
            smaller = eng.alloc_register()
            register = eng.alloc_register()
            eng.reg_alu(smaller, a, b, ALU.min)
            eng.reg_alu(register, smaller, low, ALU.max)
            return eng.snap(register, min_val=low, max_val=high)

        def bounded(eng, value, low, high):
            register = eng.alloc_register()
            eng.reg_alu(register, value, 0, ALU.add)
            return eng.snap(register, min_val=low, max_val=high)

        def block_range(eng, first, end, b):
            start = bounded(eng, first + b * BLOCK, 0, NC - 1)
            size = least(eng, end - start, BLOCK, 1, BLOCK)
            return start, size, bounded(eng, b * BLOCK + size, 1, NC)

        def chunk_range(eng, b, start, i):
            return (bounded(eng, start + i, 0, NC - 1),
                    bounded(eng, b * BLOCK + i, 0, NC - 1))

        def kept(i, t, h):
            at = i * (2 * TOKENS) + (t * TOKENS + h * HALF)
            return scores[:, :, :].rearrange("p a b -> p (a b)")[:, bass.ds(at, HALF)]

        UNITS = [(t, h) for t in range(2) for h in range(2)]

        block = ctx.enter_context(nc.Block())

        @block.sync
        def _(sp):
            sp.dma_start(mask_u[:, :].bitcast(mybir.dt.uint32), mask).then_inc(mask_in, 16)
            sp.dma_start(x_n[:, :, :], x.rearrange("(t p) d -> p t d", p=P)).then_inc(x_in, 16)
            sp.dma_start(wk[:, :], Wk).then_inc(wk_in, 16)
            first, end, blocks, chunks = load_bounds(sp)
            with sp.Fori(first, end) as j:
                sp.dma_start(keys_t[:, bass.ds(j * CHUNK, CHUNK)],
                             ctx_t[:, bass.ds(j * CHUNK, CHUNK)]).then_inc(keys_t_in, 16)
            with sp.Fori(first, end) as j:
                sp.dma_start(keys_n[:, bass.ds(j * 2, 2), :],
                             ctx_n[:, bass.ds(j * 2, 2), :]).then_inc(keys_n_in, 16)
            sp.dma_start(w_f[:, :, 0:4 * P], w13_t).then_inc(w_in, 16)
            sp.dma_start(w_f[:, :, 4 * P:6 * P], w2_t).then_inc(w_in, 16)
            for h in range(2):
                sp.wait_ge(out_ok, h + 1)
                sp.dma_start(half(out_t, h), half(out_s, h)).then_inc(out_sent, 16)
            sp.wait_ge(out_sent, 32)

        @block.gpsimd
        def _(pool):
            g = nc.gpsimd
            g.memset(ident[:, :], 0.0).then_inc(pool_k, 1)
            g.memset(ones_f[:, :], 1.0).then_inc(consts, 1)
            pool.wait_ge(pool_k, 1)
            g.affine_select(out=ident[:, :], in_=ident[:, :], compare_op=ALU.not_equal, fill=1.0, base=0,
                            pattern=[[-1, P]], channel_multiplier=1).then_inc(consts, 1)
            g.iota(chunk_no[:, 0, :], pattern=[[1, NC]], base=1, channel_multiplier=0,
                   allow_small_or_imprecise_dtypes=True).then_inc(consts, 1)
            g.iota(chunk_no[:, 1, :], pattern=[[-1, NC]], base=NC, channel_multiplier=0,
                   allow_small_or_imprecise_dtypes=True).then_inc(consts, 1)
            g.memset(neg_half[:, :], -0.5).then_inc(consts, 1)
            pool.wait_ge(mask_conv, 3)
            g.affine_select(out=key_bias[:, :], in_=key_bias0[:, :], compare_op=ALU.is_ge, fill=PADDED,
                            base=-PAD, pattern=[[P, KT]], channel_multiplier=1).then_inc(key_cols, 1)
            pool.wait_ge(wq_in, 16)
            g.tensor_copy(wq_p[0][:, :], wq[:, :]).then_inc(pool_w, 1)
            pool.wait_ge(pool_w, 1)
            g.tensor_tensor(wq_p[1][:, :], wq[:, :], f(wq_p[0][:, :]), ALU.subtract).then_inc(pool_w, 1)
            pool.wait_ge(consts, 5)
            pool.wait_ge(norm_var, 1)
            g.tensor_tensor(rstd[:, :], var[:, :], neg_half[:, :], ALU.pow).then_inc(norm_rstd, 1)
            g.memset(zeros_b[:, :], 0.0).then_inc(consts, 1)
            g.memset(run_max[:, :], LOWEST).then_inc(max_run, 2)
            g.tensor_copy(ones_r[:, :], ones_f[:, :]).then_inc(consts, 1)
            pool.wait_ge(bo_in, 16)
            pool.wait_ge(norm_x, NT)
            for i in range(NT):
                g.tensor_tensor(x_n[:, i, :], x_n[:, i, :], bo_row[:, :], ALU.add).then_inc(xb_ok, 1)
            pool.wait_ge(wv_in, 32)
            pool.wait_ge(gate_in, 16)
            for n, (w, p) in enumerate(((wv, wv_p), (wo, wo_p), (gate, gate_p))):
                g.tensor_copy(p[0][:, :], w[:, :]).then_inc(pool_w, 1)
                pool.wait_ge(pool_w, 3 + 2 * n)
                g.tensor_tensor(p[1][:, :], w[:, :], f(p[0][:, :]), ALU.subtract).then_inc(pool_w, 1)
            g.memset(earlier[:, :, :], 1.0).then_inc(pool_k, 1)
            g.memset(row_mask[:, :], 0.0).then_inc(pool_k, 1)
            pool.wait_ge(pool_k, 3)
            g.affine_select(out=earlier[:, :, :], in_=earlier[:, :, :], compare_op=ALU.is_gt, fill=0.0, base=0,
                            pattern=[[1, E], [-1, E]], channel_multiplier=0).then_inc(consts, 1)
            for n, base in enumerate((0, -E)):
                g.affine_select(out=row_mask[:, :], in_=row_mask[:, :], compare_op=ALU.not_equal, fill=1.0,
                                base=base, pattern=[[-1, E]], channel_multiplier=1).then_inc(consts, 1)
                pool.wait_ge(consts, 9 + n)

            first, end, blocks, chunks = load_bounds(pool)
            with pool.Fori(0, blocks) as b:
                start, size, done = block_range(pool, first, end, b)
                with pool.Fori(0, size) as i:
                    j, c = chunk_range(pool, b, start, i)
                    pool.wait_ge(keys_n_in, chunks * 16)
                    for t in range(2):
                        pool.wait_ge(pv, c * 4 + (2 * t + 2))
                        g.tensor_copy(v_p[0][:, t, :], keys_n[:, bass.ds(j * 2 + t, 1), :].rearrange(
                            "p a d -> p (a d)")).then_inc(pool_w, 1)
                        pool.wait_ge(pool_w, c * 2 + (9 + t))
                        at = bounded(pool, j * 2 + t, 0, KT - 1)
                        g.tensor_tensor(v_p[1][:, t, :], keys_n[:, bass.ds(at, 1), :].rearrange(
                            "p a d -> p (a d)"), f(v_p[0][:, t, :]), ALU.subtract).then_inc(v_ok, 1)

            for h in range(2):
                pool.wait_ge(norm_var, h + 2)
                g.tensor_tensor(rstd[:, h * HT:(h + 1) * HT], var[:, h * HT:(h + 1) * HT],
                                neg_half[:, 0:HT], ALU.pow).then_inc(norm_rstd, 1)

            pool.sem_inc(inner_lo, 4)
            with pool.Fori(0, E // 2) as ep:
                for u in range(8):
                    n = ep * 8 + u
                    s = u % 4
                    pool.wait_ge(inner_hi, n + 1)
                    g.tensor_tensor(p_p[1][:, s, :], inner[:, s, :], f(p_p[0][:, s, :]),
                                    ALU.subtract).then_inc(inner_lo, 1)

        @block.scalar
        def _(act):
            s = nc.scalar
            act.dma_start(wq[:, :], Wq).then_inc(wq_in, 16)
            for t, src in ((bq_c, bq), (bk_c, bk), (bv_c, bv)):
                act.dma_start(t[:, :], src).then_inc(col_in, 16)
            act.dma_start(bo_row[:, :], bo.to_broadcast([P, P])).then_inc(bo_in, 16)
            act.dma_start(wv[:, :], Wv).then_inc(wv_in, 16)
            act.dma_start(wo[:, :], Wo).then_inc(wv_in, 16)
            act.dma_start(gate[:, :], gate_t).then_inc(gate_in, 16)

            for h in range(2):
                act.wait_ge(tr_ps, h + 1)
                s.activation(half(xt_p[0], h), bank[4 + h][:, :], ACT.Copy).then_inc(xt_hi, 1)
            act.wait_ge(col_in, 48)
            for h in range(2):
                act.wait_ge(q_ps, h + 1)
                s.activation(half(q_p[0], h), bank[h][:, :], ACT.Identity, bias=bq_c[:, :]).then_inc(q_hi, 1)
            first, end, blocks, chunks = load_bounds(act)
            act.wait_ge(key_cols, 1)
            act.sem_inc(score_kept, 4)
            act.sem_inc(alpha_ok, 2)

            def key_hi(c, t):
                act.wait_ge(key_ps, c + 1)
                if t == 1:
                    act.wait_ge(score_ps, c * 4 + 4)
                    act.wait_ge(k_lo, c * 2 + 1)
                s.activation(k_p[0][:, t, :], bank[KEY_BANK][:, t * P:(t + 1) * P], ACT.Identity,
                             bias=bk_c[:, :]).then_inc(k_hi, 1)

            for t in range(2):
                act.wait_ge(key_ps, 1)
                if t == 1:
                    act.wait_ge(k_lo, 1)
                s.activation(k_p[0][:, t, :], bank[KEY_BANK][:, t * P:(t + 1) * P], ACT.Identity,
                             bias=bk_c[:, :]).then_inc(k_hi, 1)
            with act.Fori(0, blocks) as b:
                start, size, done = block_range(act, first, end, b)
                with act.Fori(0, size) as i:
                    j, c = chunk_range(act, b, start, i)
                    for u, (t, h) in enumerate(UNITS):
                        act.wait_ge(score_ps, c * 4 + (u + 5))
                        s.activation(kept(i, t, h), bank[SCORE_BANK[u]][:, :], ACT.Identity,
                                     bias=key_bias[:, bass.ds(j * 2 + t, 1)],
                                     scale=key_scale[:, bass.ds(j * 2 + t, 1)]).then_inc(score_kept, 1)
                        if u == 1:
                            key_hi(c + 1, 0)
                    key_hi(c + 1, 1)
                with act.If(b > 0):
                    for h in range(2):
                        act.wait_ge(old_diff, b * 2 + (h + 1))
                        s.activation(half(alpha, h), half(alpha, h), ACT.Exp).then_inc(alpha_ok, 1)
                with act.Fori(0, size) as i:
                    j, c = chunk_range(act, b, start, i)
                    for u, (t, h) in enumerate(UNITS):
                        act.wait_ge(prob_lo, c * 4 + (u + 1))
                        act.wait_ge(shifted, c * 4 + (u + 1))
                        s.activation(bank[4 + u][:, :], kept(i, t, h), ACT.Exp).then_inc(prob, 1)
                        act.wait_ge(prob, c * 4 + (u + 1))
                        act.wait_ge(pv, c * 4 + (u + 1))
                        s.activation(p_p[0][:, u, :], bank[4 + u][:, :], ACT.Copy).then_inc(prob_hi, 1)

            for h in range(2):
                act.wait_ge(o_norm, h + 1)
                s.activation(half(xt_p[0], h), half(o_n, h), ACT.Copy).then_inc(o_hi, 1)
            for h in range(2):
                act.wait_ge(val_ps, h + 1)
                s.activation(half(q_p[0], h), bank[4 + h][:, :], ACT.Identity, bias=bv_c[:, :]).then_inc(val_hi, 1)
            for h in range(2):
                act.wait_ge(tr_ps, h + 3)
                s.activation(half(xt_p[0], h), bank[4 + h][:, :], ACT.Copy).then_inc(xt_hi, 1)
                act.wait_ge(x1_tr_ps, h + 1)
                s.activation(half(x1_t, h), bank[6 + h][:, :], ACT.Copy).then_inc(x1_t_ok, 1)
            act.wait_ge(logit_sub, 1)
            s.activation(r8[1], r8[0], ACT.Exp).then_inc(logit_exp, 1)

            act.wait_ge(w_in, 32)
            s.activation(w_p[0][0][:, :], w_f[:, 0, :], ACT.Copy).then_inc(w_hi, 1)
            with act.Fori(0, E // 2) as ep:
                for u in range(8):
                    n = ep * 8 + u
                    if u % 4 == 2:
                        q = 1 - u // 4
                        nxt = least(act, ep * 2 + (1 + u // 4), E - 1, 1, E - 1)
                        act.wait_ge(down, n + 2)
                        s.activation(w_p[q][0][:, :], w_f[:, bass.ds(nxt, 1), :].rearrange("p a d -> p (a d)"),
                                     ACT.Copy).then_inc(w_hi, 1)
                    act.wait_ge(gate_ps, n + 1)
                    act.wait_ge(silc_ok, n + 1)
                    s.activation(silu[:, u % 2, :], bank[4 + 2 * (u % 2)][:, :], ACT.Silu).then_inc(silu_ok, 1)
                    act.wait_ge(inner_ok, n + 3)
                    act.wait_ge(down, n + 1)
                    s.activation(p_p[0][:, u % 4, :], inner[:, u % 4, :], ACT.Copy).then_inc(inner_hi, 1)

        @block.vector
        def _(dve):
            v = nc.vector
            chain = Chain(dve, dve_chain)
            dve.wait_ge(mask_in, 16)
            v.tensor_copy(mask_f[:, :], mask_u[:, :]).then_inc(mask_conv, 1)
            dve.wait_ge(mask_conv, 1)
            v.tensor_scalar(key_scale[:, :], mask_f[:, :], SCALE, None, ALU.mult).then_inc(mask_conv, 1)
            v.tensor_scalar(key_bias0[:, :], mask_f[:, :], 1.0, -MASKED, ALU.subtract, ALU.mult).then_inc(mask_conv, 1)

            def norm_stats(src, i0, i1):
                for i in range(i0, i1):
                    chain.link(v.bn_stats(stats[:, i, :], src[:, i, :]))
                chain.settle()
                for i in range(i0, i1):
                    chain.link(v.bn_aggr(mv[:, i, :], stats[:, i, :]))
                chain.settle()
                v.tensor_scalar(var[:, i0:i1], mv[:, i0:i1, 1], EPS, None, ALU.add).then_inc(norm_var, 1)

            def norm_apply(src, i0, i1):
                for i in range(i0, i1):
                    v.tensor_scalar(xn[:, i, :], src[:, i, :], mv[:, i, 0:1], rstd[:, i:i + 1],
                                    ALU.subtract, ALU.mult).then_inc(norm_x, 1)

            dve.wait_ge(count_ps, 1)
            dve.wait_ge(consts, 4)
            chain.step(v.tensor_reduce(count[:, :], bank[6][0:1, 0:KT].rearrange("p (c t) -> p c t", t=2),
                                       X, ALU.add))
            chain.step(v.tensor_scalar(count[:, :], count[:, :], 0.0, None, ALU.is_gt))
            for i in range(2):
                chain.link(v.tensor_tensor(marked[:, i, :], count[:, :], chunk_no[:, i, :], ALU.mult))
            chain.settle()
            chain.step(v.tensor_reduce(edge[:, :], marked[:, :, :], X, ALU.max))
            chain.step(v.tensor_scalar(none[:, :], edge[:, :], 0.0, float(NC), ALU.is_equal, ALU.mult))
            chain.step(v.tensor_tensor(edge2[:, :], edge[:, :], none[:, :], ALU.add))
            chain.link(v.tensor_scalar(span[:, 0:1], edge2[:, 1:2], -1.0, float(NC), ALU.mult, ALU.add))
            chain.link(v.tensor_copy(span[:, 1:2], edge2[:, 0:1]))
            chain.settle()
            chain.step(v.tensor_tensor(span[:, 3:4], span[:, 1:2], span[:, 0:1], ALU.subtract))
            for i in range(3):
                chain.link(v.tensor_scalar(over[:, i:i + 1], span[:, 3:4], float(BLOCK * (i + 1)), None, ALU.is_gt))
            chain.settle()
            chain.step(v.tensor_reduce(span[:, 2:3], over[:, :], X, ALU.add))
            chain.step(v.tensor_scalar(span[:, 2:3], span[:, 2:3], 1.0, None, ALU.add))
            v.tensor_copy(bounds[:, :], span[:, :]).then_inc(bounds_ok, 1)

            dve.wait_ge(x_in, 16)
            norm_stats(x_n, 0, NT)
            dve.wait_ge(norm_rstd, 1)
            norm_apply(x_n, 0, NT)
            for h in range(2):
                dve.wait_ge(xt_hi, h + 1)
                v.tensor_tensor(half(xt_p[1], h), bank[4 + h][:, :], f(half(xt_p[0], h)),
                                ALU.subtract).then_inc(xt_lo, 1)
            for h in range(2):
                dve.wait_ge(q_hi, h + 1)
                v.scalar_tensor_tensor(half(q_p[1], h), bank[h][:, :], bq_c[:, :], f(half(q_p[0], h)),
                                       ALU.add, ALU.subtract).then_inc(q_lo, 1)

            first, end, blocks, chunks = load_bounds(dve)

            def key_lo(t):
                v.scalar_tensor_tensor(k_p[1][:, t, :], bank[KEY_BANK][:, t * P:(t + 1) * P], bk_c[:, :],
                                       f(k_p[0][:, t, :]), ALU.add, ALU.subtract).then_inc(k_lo, 1)

            for t in range(2):
                dve.wait_ge(k_hi, t + 1)
                key_lo(t)
            dve.wait_ge(acc_zero, 1)
            dve.sem_inc(prob_lo, 4)
            dve.sem_inc(old_diff, 2)
            with dve.Fori(0, blocks) as b:
                start, size, done = block_range(dve, first, end, b)
                with dve.Fori(0, size) as i:
                    j, c = chunk_range(dve, b, start, i)
                    for u, (t, h) in enumerate(UNITS):
                        dve.wait_ge(score_kept, c * 4 + (u + 5))
                        dve.wait_ge(max_run, c * 4 + (u + 1))
                        v.tensor_tensor(half(run_max, h), half(run_max, h), kept(i, t, h),
                                        ALU.max).then_inc(max_run, 1)
                        if u == 1:
                            dve.wait_ge(k_hi, c * 2 + 3)
                            key_lo(0)
                    dve.wait_ge(k_hi, c * 2 + 4)
                    key_lo(1)
                for h in range(2):
                    dve.wait_ge(max_tr, b * 2 + (h + 1))
                    v.tensor_reduce(max_col[:, h * HT:(h + 1) * HT],
                                    bank[4 + h][:, :].rearrange("p (i k) -> p i k", k=P), X, ALU.max)\
                        .then_inc(max_cols, 1)
                    dve.wait_ge(max_cols, b * 6 + (3 * h + 1))
                    for m in range(h * HT, (h + 1) * HT):
                        last = v.tensor_scalar(max_mat[:, m, :], ident[:, :],
                                               max_col[:, m:m + 1], None, ALU.mult)
                    last.then_inc(max_cols, 2)
                with dve.If(b > 0):
                    for h in range(2):
                        dve.wait_ge(max_ps, b * 2 + (h + 1))
                        v.tensor_tensor(half(alpha, h), half(max_b, h), bank[6 + h][:, :],
                                        ALU.subtract).then_inc(old_diff, 1)
                    for h in range(2):
                        dve.wait_ge(alpha_ok, b * 2 + (h + 1))
                        for acc in (h, 2 + h):
                            v.tensor_tensor(bank[acc][:, :], bank[acc][:, :], half(alpha, h), ALU.mult)\
                                .then_inc(acc_zero, 1)
                for h in range(2):
                    dve.wait_ge(max_ps, b * 2 + (h + 1))
                    v.tensor_copy(half(max_b, h), bank[6 + h][:, :]).then_inc(max_ok, 1)

                def low(n, u):
                    dve.wait_ge(prob_hi, n)
                    v.tensor_tensor(p_p[1][:, u, :], bank[4 + u][:, :], f(p_p[0][:, u, :]),
                                    ALU.subtract).then_inc(prob_lo, 1)

                with dve.Fori(0, size) as i:
                    j, c = chunk_range(dve, b, start, i)
                    for u, (t, h) in enumerate(UNITS):
                        at = kept(i, t, h)
                        if u < 2:
                            dve.wait_ge(max_ok, b * 2 + (h + 1))
                        v.tensor_tensor(at, at, half(max_b, h), ALU.subtract).then_inc(shifted, 1)
                        if u >= 1:
                            low(c * 4 + u, u - 1)
                    low(c * 4 + 4, 3)

            dve.wait_ge(attn_end, 1)
            for h in range(2):
                chain.step(v.reciprocal(half(rsum, h), bank[2 + h][:, :]))
                v.tensor_tensor(half(o_n, h), bank[h][:, :], half(rsum, h), ALU.mult).then_inc(o_norm, 1)
            for h in range(2):
                dve.wait_ge(o_hi, h + 1)
                v.tensor_tensor(half(xt_p[1], h), half(o_n, h), f(half(xt_p[0], h)),
                                ALU.subtract).then_inc(o_lo, 1)
            for h in range(2):
                dve.wait_ge(val_hi, h + 1)
                v.scalar_tensor_tensor(half(q_p[1], h), bank[4 + h][:, :], bv_c[:, :], f(half(q_p[0], h)),
                                       ALU.add, ALU.subtract).then_inc(val_lo, 1)
            dve.wait_ge(xb_ok, NT)
            for h in range(2):
                dve.wait_ge(attn_ps, h + 1)
                v.tensor_tensor(x1[:, h * HT:(h + 1) * HT, :].rearrange("p t d -> p (t d)"), bank[6 + h][:, :],
                                half(x_n[:, :, :].rearrange("p t d -> p (t d)"), h), ALU.add).then_inc(x1_ok, 1)
                dve.wait_ge(x1_ok, h + 1)
                norm_stats(x1, h * HT, (h + 1) * HT)
                dve.wait_ge(norm_rstd, h + 2)
                norm_apply(x1, h * HT, (h + 1) * HT)
            for h in range(2):
                dve.wait_ge(xt_hi, h + 3)
                v.tensor_tensor(half(xt_p[1], h), bank[4 + h][:, :], f(half(xt_p[0], h)),
                                ALU.subtract).then_inc(xt_lo, 1)

            dve.wait_ge(logit_ps, 1)
            logits = bank[2][:, 0:NT * E].rearrange("p (t e) -> p t e", e=E)
            chain.step(v.tensor_reduce(r1[0], logits, X, ALU.max))
            v.tensor_tensor(r8[0], logits, r1[0].unsqueeze(2).to_broadcast([P, NT, E]),
                            ALU.subtract).then_inc(logit_sub, 1)
            dve.wait_ge(w_hi, 1)
            v.tensor_tensor(w_p[0][1][:, :], w_f[:, 0, :], f(w_p[0][0][:, :]), ALU.subtract).then_inc(w_lo, 1)
            dve.wait_ge(logit_exp, 1)
            chain.step(v.tensor_reduce(r1[1], r8[1], X, ALU.add))
            chain.step(v.reciprocal(r1[2], r1[1]))
            chain.step(v.tensor_tensor(r8[2], r8[1], r1[2].unsqueeze(2).to_broadcast(
                [P, NT, E]), ALU.mult))
            chain.step(v.tensor_reduce(g4[0], r8[2].rearrange("p t (g k) -> p t g k", k=EG),
                                       X, ALU.max))

            def keep_top(keep, val, n):
                first_i = pair[0][:, :, 0:n, 0:n]
                second = pair[1][:, :, 0:n, 0:n]
                mine = val.unsqueeze(3).to_broadcast([P, NT, n, n])
                other = val.unsqueeze(2).to_broadcast([P, NT, n, n])
                chain.link(v.tensor_tensor(first_i, other, mine, ALU.is_equal))
                chain.link(v.tensor_tensor(second, other, mine, ALU.is_gt))
                chain.settle()
                chain.step(v.tensor_tensor(first_i, first_i, earlier[:, 0:n, 0:n].unsqueeze(1).to_broadcast(
                    [P, NT, n, n]), ALU.mult))
                chain.step(v.tensor_tensor(first_i, first_i, second, ALU.add))
                chain.step(v.tensor_reduce(keep, first_i, X, ALU.add))
                chain.step(v.tensor_scalar(keep, keep, float(TOP), None, ALU.is_lt))

            keep_top(g4[1], g4[0], G)
            for k in range(EG):
                chain.link(v.tensor_tensor(r8[3].rearrange("p t (g k) -> p t g k", k=EG)[:, :, :, k],
                                           r8[2].rearrange("p t (g k) -> p t g k", k=EG)[:, :, :, k],
                                           g4[1], ALU.mult))
            chain.settle()
            keep_top(r8[4], r8[3], E)
            chain.step(v.tensor_tensor(r8[5], r8[3], r8[4], ALU.mult))
            chain.step(v.tensor_reduce(r1[0], r8[5], X, ALU.add))
            chain.step(v.reciprocal(r1[1], r1[0]))
            chain.step(v.tensor_tensor(r8[6], r8[5], r1[1].unsqueeze(2).to_broadcast(
                [P, NT, E]), ALU.mult))
            hi = r8[7].bitcast(F32R)
            chain.step(v.tensor_copy(hi, r8[6]))
            v.tensor_copy(comb[:, :, 0:E], r8[7]).then_inc(comb_ok, 1)
            v.tensor_tensor(comb[:, :, E:2 * E], r8[6], r8[7], ALU.subtract).then_inc(comb_ok, 1)
            for h in range(2):
                dve.wait_ge(comb_ps, h + 1)
                v.tensor_copy(half(comb_t, h), bank[2 + h][0:2 * E, :]).then_inc(comb_t_ok, 1)
            dve.wait_ge(comb_t_ok, 2)
            v.tensor_scalar(comb_e[0], comb_t, row_mask[:, 0:1], None, ALU.mult).then_inc(comb_e_ok, 1)
            dve.sem_inc(silc_ok, 2)
            dve.sem_inc(inner_ok, 2)
            with dve.Fori(0, E // 2) as ep:
                for u in range(8):
                    n = ep * 8 + u
                    h = (u // 2) % 2
                    if u % 4 == 0:
                        q = 1 - u // 4
                        nxt = least(dve, ep * 2 + (1 + u // 4), E - 1, 1, E - 1)
                        v.tensor_scalar(comb_e[q], comb_t, row_mask[:, bass.ds(nxt, 1)], None,
                                        ALU.mult).then_inc(comb_e_ok, 1)
                    dve.wait_ge(silu_ok, n + 1)
                    dve.wait_ge(comb_b, ep * 4 + (u // 2 + 1))
                    v.tensor_tensor(silc[:, u % 2, :], silu[:, u % 2, :], bank[2 + h][:, :],
                                    ALU.mult).then_inc(silc_ok, 1)
                    dve.wait_ge(up_ps, n + 1)
                    dve.wait_ge(silc_ok, n + 3)
                    dve.wait_ge(inner_lo, n + 1)
                    v.tensor_tensor(inner[:, u % 4, :], silc[:, u % 2, :], bank[5 + 2 * (u % 2)][:, :],
                                    ALU.mult).then_inc(inner_ok, 1)
                    if u % 4 == 2:
                        q = 1 - u // 4
                        nxt = least(dve, ep * 2 + (1 + u // 4), E - 1, 1, E - 1)
                        dve.wait_ge(w_hi, ep * 2 + (2 + u // 4))
                        v.tensor_tensor(w_p[q][1][:, :], w_f[:, bass.ds(nxt, 1), :].rearrange("p a d -> p (a d)"),
                                        f(w_p[q][0][:, :]), ALU.subtract).then_inc(w_lo, 1)
            dve.wait_ge(x1_t_ok, 2)
            dve.wait_ge(y_end, 1)
            for h in range(2):
                v.tensor_tensor(half(out_s, h), bank[h][:, :], half(x1_t, h), ALU.add).then_inc(out_ok, 1)

        @block.tensor
        def _(pe):
            mm = nc.tensor.matmul

            def product(out, lhs, rhs, start=True, stop=True):
                grouped = dict(skip_group_check=not (start and stop))
                mm(out, lhs[0], rhs[0], start=start, stop=False, **grouped)
                mm(out, lhs[1], rhs[0], start=False, stop=False, **grouped)
                return mm(out, lhs[0], rhs[1], start=False, stop=stop, **grouped)

            def halves(t, h):
                return tuple(half(x_, h) for x_ in t)

            pe.wait_ge(consts, 1)
            pe.wait_ge(mask_conv, 1)
            mm(bank[6][0:1, 0:KT], ones_f[:, 0:1], mask_f[:, :], start=True, stop=True).then_inc(count_ps, 1)
            pe.wait_ge(consts, 2)
            for h in range(2):
                for i in range(HT):
                    pe.wait_ge(norm_x, h * HT + i + 1)
                    last = nc.tensor.transpose(bank[4 + h][:, i * P:(i + 1) * P], xn[:, h * HT + i, :], ident[:, :])
                last.then_inc(tr_ps, 1)
            pe.wait_ge(pool_w, 2)
            for h in range(2):
                pe.wait_ge(xt_lo, h + 1)
                product(bank[h][:, :], [w[:, :] for w in wq_p], halves(xt_p, h)).then_inc(q_ps, 1)

            first, end, blocks, chunks = load_bounds(pe)
            pe.wait_ge(wk_in, 16)
            pe.wait_ge(keys_t_in, chunks * 16)
            mm(bank[KEY_BANK][:, 0:CHUNK], wk[:, :], keys_t[:, bass.ds(first * CHUNK, CHUNK)],
               start=True, stop=True).then_inc(key_ps, 1)
            pe.wait_ge(consts, 7)
            pe.wait_ge(q_lo, 2)
            for n in range(4):
                last = mm(bank[n][:, :], zeros_b[:, 0:P], zeros_b[:, :], start=True, stop=False,
                          skip_group_check=True)
            last.then_inc(acc_zero, 1)
            pe.sem_inc(score_ps, 4)
            pe.sem_inc(pv, 4)
            with pe.Fori(0, blocks) as b:
                start, size, done = block_range(pe, first, end, b)
                with pe.Fori(0, size) as i:
                    j, c = chunk_range(pe, b, start, i)
                    for u, (t, h) in enumerate(UNITS):
                        if u == 0:
                            pe.wait_ge(prob_lo, b * (4 * BLOCK) + 4)
                        if h == 0:
                            pe.wait_ge(k_lo, c * 2 + (t + 1))
                        if u == 2:
                            nxt = least(pe, j + 1, end - 1, 0, NC - 1)
                            mm(bank[KEY_BANK][:, 0:CHUNK], wk[:, :], keys_t[:, bass.ds(nxt * CHUNK, CHUNK)],
                               start=True, stop=True).then_inc(key_ps, 1)
                        pe.wait_ge(score_kept, c * 4 + SCORE_WAIT[u])
                        product(bank[SCORE_BANK[u]][:, :], [k[:, t, :] for k in k_p],
                                halves(q_p, h)).then_inc(score_ps, 1)
                for h in range(2):
                    pe.wait_ge(max_run, done * 4 + (h + 1))
                    for i in range(HT):
                        last = nc.tensor.transpose(bank[4 + h][:, i * P:(i + 1) * P],
                                                   tile(run_max, h * HT + i), ident[:, :])
                    last.then_inc(max_tr, 1)
                pe.wait_ge(k_lo, done * 2 + 2)
                for h in range(2):
                    pe.wait_ge(max_cols, b * 6 + (3 * h + 3))
                    for i in range(HT):
                        last = mm(bank[6 + h][:, i * P:(i + 1) * P], ones_f[:, :], max_mat[:, h * HT + i, :],
                                  start=True, stop=True)
                    last.then_inc(max_ps, 1)
                with pe.Fori(0, size) as i:
                    j, c = chunk_range(pe, b, start, i)
                    for u, (t, h) in enumerate(UNITS):
                        if u == 0:
                            pe.wait_ge(acc_zero, b * 4 + 1)
                        if h == 0:
                            pe.wait_ge(v_ok, c * 2 + (t + 1))
                        pe.wait_ge(prob_lo, c * 4 + (u + 5))
                        product(bank[h][:, :], [w[:, t, :] for w in v_p], [w[:, u, :] for w in p_p],
                                start=False, stop=False)
                        for w in p_p:
                            last = mm(bank[2 + h][:, :], ones_r[:, :], w[:, u, :], start=False, stop=False,
                                      skip_group_check=True)
                        last.then_inc(pv, 1)
            for n in range(4):
                last = mm(bank[n][:, :], zeros_b[:, 0:P], zeros_b[:, :], start=False, stop=True,
                          skip_group_check=True)
            last.then_inc(attn_end, 1)

            pe.wait_ge(pool_w, 8)
            for h in range(2):
                pe.wait_ge(o_lo, h + 1)
                product(bank[4 + h][:, :], [w[:, :] for w in wv_p], halves(xt_p, h)).then_inc(val_ps, 1)
            for h in range(2):
                pe.wait_ge(val_lo, h + 1)
                for i in range(HT):
                    last = product(bank[6 + h][:, i * P:(i + 1) * P], [tile(w, h * HT + i) for w in q_p],
                                   [w[:, :] for w in wo_p])
                last.then_inc(attn_ps, 1)
            for h in range(2):
                for i in range(HT):
                    pe.wait_ge(norm_x, NT + h * HT + i + 1)
                    last = nc.tensor.transpose(bank[4 + h][:, i * P:(i + 1) * P], xn[:, h * HT + i, :], ident[:, :])
                last.then_inc(tr_ps, 1)
                for i in range(HT):
                    last = nc.tensor.transpose(bank[6 + h][:, i * P:(i + 1) * P], x1[:, h * HT + i, :], ident[:, :])
                last.then_inc(x1_tr_ps, 1)
            for i in range(NT):
                if i % HT == 0:
                    pe.wait_ge(xt_lo, 3 + i // HT)
                last = product(bank[2][:, i * E:(i + 1) * E], [tile(w, i) for w in xt_p], [w[:, :] for w in gate_p])
            last.then_inc(logit_ps, 1)
            for h in range(2):
                mm(bank[h][:, :], zeros_b[:, 0:P], zeros_b[:, :], start=True, stop=False, skip_group_check=True)

            def gate_up(u):
                h, it, q = (u // 2) % 2, u % 2, u // 4
                product(bank[4 + 2 * (u % 2)][:, :], [tile(w, it) for w in w_p[q]],
                        halves(xt_p, h)).then_inc(gate_ps, 1)
                product(bank[5 + 2 * (u % 2)][:, :], [tile(w, 2 + it) for w in w_p[q]],
                        halves(xt_p, h)).then_inc(up_ps, 1)

            def down_product(u, low_parts):
                h, it, q = (u // 2) % 2, u % 2, u // 4
                pe.wait_ge(inner_lo, low_parts)
                product(bank[h][:, :], [tile(w, 4 + it) for w in w_p[q]], [w[:, u % 4, :] for w in p_p],
                        start=False, stop=False).then_inc(down, 1)

            pe.wait_ge(x1_t_ok, 2)
            pe.wait_ge(comb_ok, 2)
            for h in range(2):
                for i in range(HT):
                    last = nc.tensor.transpose(bank[2 + h][0:2 * E, i * P:(i + 1) * P], comb[:, h * HT + i, :],
                                               ident[:, :])
                last.then_inc(comb_ps, 1)
            pe.wait_ge(comb_t_ok, 2)

            def combine(q, h, n):
                pe.wait_ge(comb_e_ok, n)
                mm(bank[2 + h][:, :], ones_r[0:2 * E, :], half(comb_e[q], h), start=True,
                   stop=True).then_inc(comb_b, 1)

            combine(0, 0, 1)
            pe.sem_inc(down, 4)
            with pe.Fori(0, E // 2) as ep:
                for u in range(8):
                    n = ep * 8 + u
                    if u % 4 == 0:
                        pe.wait_ge(w_lo, ep * 2 + (u // 4 + 1))
                    pe.wait_ge(inner_ok, n + 1)
                    if u % 2 == 0:
                        h_next = 1 - (u // 2) % 2
                        q_next = ((u + 2) // 4) % 2
                        pe.wait_ge(silc_ok, n + 2)
                        combine(q_next, h_next, ep * 2 + (1 + (u + 2) // 4))
                    gate_up(u)
                    if u >= 2:
                        down_product(u - 2, ep * 8 + (u + 3))
                    else:
                        with pe.If(ep > 0):
                            down_product(u + 6, ep * 8 + (u + 3))
            for u in (6, 7):
                down_product(u, (E // 2 - 1) * 8 + u + 5)
            for h in range(2):
                last = mm(bank[h][:, :], zeros_b[:, 0:P], zeros_b[:, :], start=False, stop=True,
                          skip_group_check=True)
            last.then_inc(y_end, 1)


_INS = ["x", "mask", "ctx_t", "ctx_n", "Wq", "bq", "Wk", "bk", "Wv", "bv", "Wo", "bo", "gate_t", "w13_t", "w2_t"]


def kernel(**inputs):
    import numpy as np
    import concourse.bacc as bacc
    from concourse.bass_utils import run_bass_kernel_spmd

    a = {k.replace("L0_xattn_", "").replace("L0_ffn_", ""): np.asarray(v) for k, v in inputs.items()}
    context = a["ctx_1024"][0]
    keys, width = context.shape
    whole = -(-keys // CHUNK) * CHUNK
    padded = np.zeros((whole, width), context.dtype)
    padded[whole - keys:] = context
    mask = np.zeros(whole, np.uint8)
    mask[whole - keys:] = a["mask_BxS2_bk0"][0].view(np.uint8)
    experts, _, inter = a["w2_weight"].shape
    data = {
        "x": a["x"][0],
        "mask": np.ascontiguousarray(mask.reshape(-1, P).T).view(np.uint32),
        "ctx_t": padded.T,
        "ctx_n": padded.reshape(-1, P, width).transpose(1, 0, 2),
        "gate_t": a["gate_w"].T,
        "w13_t": a["w13_weight"].transpose(2, 0, 1),
        "w2_t": a["w2_weight"].reshape(experts, width, inter // P, P).transpose(3, 0, 2, 1).reshape(P, experts, -1),
    }
    for name in ("Wq", "Wk", "Wv", "Wo"):
        data[name] = a[name]
    for name in ("bq", "bk", "bv"):
        data[name] = a[name].reshape(P, 1)
    data["bo"] = a["bo"].reshape(1, P)

    nc = bacc.Bacc("TRN2", target_bir_lowering=False, num_devices=1)
    arrays, args = {}, []
    for name in _INS:
        array = np.ascontiguousarray(data[name])
        arrays[f"in_{name}"] = array
        args.append(nc.dram_tensor(f"in_{name}", array.shape, mybir.dt.from_np(array.dtype),
                                   kind="ExternalInput").ap())
    tokens = data["x"].shape[0]
    out = nc.dram_tensor("out_t", (width, tokens), F32, kind="ExternalOutput").ap()
    xattn_ffn(nc, keys, *args, out)
    result = run_bass_kernel_spmd(nc, [arrays], core_ids=[0])
    return np.ascontiguousarray(result.results[0]["out_t"].T).reshape(1, tokens, width)
```

```python
from contextlib import ExitStack

import concourse.bass as bass
from concourse import mybir

F32 = mybir.dt.float32
F32R = mybir.dt.float32r
BF16 = mybir.dt.bfloat16
I32 = mybir.dt.int32
ALU = mybir.AluOpType
ACT = mybir.ActivationFunctionType
X = mybir.AxisListType.X

P = 128
HALF = 512
CHUNK = 2 * P
MASKED = -1.0e9
PADDED = -3.0e9
LOWEST = -3.0e38
EPS = 1e-5
BLOCK = 7
FILL_MAXIMA, FILL_SHIFT, FILL_NORM, FILL_ROUTING, FILL_COMBINE = 6, 12, 20, 26, 4
SCORE_BANK = (4, 5, 6, 7)
KEY_BANK = 6



class Chain:

    def __init__(self, engine, sem):
        self.engine, self.sem, self.value = engine, sem, 0

    def link(self, instruction):
        instruction.then_inc(self.sem, 1)
        self.value += 1

    def settle(self):
        self.engine.wait_ge(self.sem, self.value)

    def step(self, instruction):
        self.link(instruction)
        self.settle()


def xattn_ffn(nc, keys, x, mask, ctx_t, ctx_n, Wq, bq, Wk, bk, Wv, bv, Wo, bo, gate_t, w13_t, w2_t, out_t):
    TOKENS = x.shape[0]
    NT = TOKENS // P
    HT = HALF // P
    KT = 4 * mask.shape[1]
    NC = KT // 2
    PAD = ctx_t.shape[1] - keys
    E = w13_t.shape[1]
    SCALE = float(P) ** -0.5
    EG = 2
    G = E // EG
    TOP = 2
    assert TOKENS == 2 * HALF and ctx_t.shape[1] == KT * P and PAD >= 0

    with ExitStack() as ctx:
        def sb(name, shape, dt=F32):
            return ctx.enter_context(nc.sbuf_tensor(name, shape, dt))

        def sem(name):
            return ctx.enter_context(nc.semaphore(name))

        bank = [ctx.enter_context(nc.psum_tensor(f"bank{i}", [P, HALF], F32)) for i in range(8)]

        ident = sb("ident", [P, P])
        ones_f = sb("ones_f", [P, P])
        ones_r = sb("ones_r", [P, P], F32R)
        zeros_b = sb("zeros_b", [P, P], BF16)
        neg_half = sb("neg_half", [P, NT])
        chunk_no = sb("chunk_no", [1, 2, NC])
        earlier = sb("earlier", [P, E, E], BF16)
        row_mask = sb("row_mask", [2 * E, E])

        x_n = sb("x_n", [P, NT, P])
        bo_row = sb("bo_row", [P, P])
        mask_u = sb("mask_u", [P, KT], mybir.dt.uint8)
        keys_t = sb("keys_t", [P, KT * P])
        keys_n = sb("keys_n", [P, KT, P])
        k_s = sb("k_s", [P, CHUNK])
        wq = k_s[:, 0:P]
        wk, wv, wo = (sb(n, [P, P]) for n in ("wk", "wv", "wo"))
        bq_c, bk_c, bv_c = (sb(n, [P, 1]) for n in ("bq_c", "bk_c", "bv_c"))
        gate = sb("gate", [P, E])
        w_f = sb("w_f", [P, E, 6 * P])

        def parts(name, shape):
            return sb(name + "_hi", shape, F32R), sb(name + "_lo", shape, F32R)

        wq_p, wv_p, wo_p = parts("wq_p", [P, P]), parts("wv_p", [P, P]), parts("wo_p", [P, P])
        gate_p = parts("gate_p", [P, E])
        xt_p = parts("xt_p", [P, TOKENS])
        q_p = parts("q_p", [P, TOKENS])
        zero_col = sb("zero_col", [P, 1])
        k_p = parts("k_p", [P, 2, P])
        v_p = parts("v_p", [P, 2, P])
        p_p = parts("p_p", [P, 4, HALF])
        w_p = [parts(f"w_p{i}", [P, 6 * P]) for i in range(2)]
        pick = [sb(f"pick{i}", [2 * E, P], F32R) for i in range(2)]
        warm = sb("warm", [1, 1])
        inv_sum = sb("inv_sum", [P, NT])

        stats = sb("stats", [P, NT, 6])
        mv = sb("mv", [P, NT, 2])
        var = sb("var", [P, NT])
        rstd = sb("rstd", [P, NT])
        xn = sb("xn", [P, NT, P])
        mask_f = sb("mask_f", [P, KT])
        key_scale = sb("key_scale", [P, KT])
        key_bias0 = sb("key_bias0", [P, KT])
        key_bias = sb("key_bias", [P, KT])
        count = sb("count", [1, NC])
        marked = sb("marked", [1, 2, NC])
        edge = sb("edge", [1, 2])
        none = sb("none", [1, 2])
        edge2 = sb("edge2", [1, 2])
        span = sb("span", [1, 4])
        over = sb("over", [1, 3])
        bounds = sb("bounds", [1, 4], I32)
        scores = sb("scores", [P, 2 * BLOCK, TOKENS])
        run_max = sb("run_max", [P, TOKENS])
        max_col = sb("max_col", [P, NT])
        max_mat = xn
        max_b = sb("max_b", [P, TOKENS])
        alpha = xn[:, :, :].rearrange("p a b -> p (a b)")
        late_at = [0]

        def late(*shape):
            size = 1
            for n in shape:
                size *= n
            at = late_at[0]
            late_at[0] += size
            assert late_at[0] <= 2 * BLOCK * TOKENS
            flat = scores[:, :, :].rearrange("p a b -> p (a b)")[:, at:at + size]
            if len(shape) == 1:
                return flat
            names = "abc"[:len(shape)]
            return flat.rearrange(f"p ({' '.join(names)}) -> p {' '.join(names)}",
                                  **dict(zip(names[1:], shape[1:])))

        sum_diag = late(NT, P)
        sum_col = late(NT)
        bv_mat = k_s[:, 0:P]
        x1 = late(NT, P)
        x1_t = late(TOKENS)
        out_s = late(TOKENS)
        r8 = [late(NT, E) for i in range(8)]
        r1 = [late(NT) for i in range(3)]
        g4 = [late(NT, G) for i in range(3)]
        pair = [late(NT, E, E // 2).bitcast(BF16) for i in range(2)]
        comb = late(NT, 2 * E)
        comb_rows = q_p[0][0:2 * E, :]
        silu = late(2, HALF)
        silc = late(2, HALF)
        inner = late(4, HALF)

        (mask_in, x_in, wq_in, wk_in, wv_in, col_in, gate_in, w_in, bo_in, first_keys_in, keys_t_in, keys_n_in,
         out_sent, consts, zero_ok, mask_conv, key_cols, count_ps, bounds_ok, pool_w, pool_k, norm_var, norm_rstd,
         norm_x, tr_ps, xt_hi, xt_lo, q_ps, q_hi, q_lo, acc_zero, key_ps, key_kept, k_hi, k_lo, score_ps, score_kept,
         max_run, max_tr, max_cols, max_diag_a, max_diag_v, max_ps, max_ok, max_ok_a, old_diff, alpha_ok, shifted,
         shifted_pool, prob, prob_hi, prob_lo, v_hi, v_ok, pv, attn_end, diag_ok, sum_ok, bv_ok, bvo_ps, bvo_ok,
         inv_ok, o_hi, o_lo, val_ps, val_hi, val_lo, attn_ps, x1_ok, x1_tr_ps, x1_t_ok, gate_ok, logit_ps, logit_exp,
         logit_sub, comb_ok, comb_ps, comb_t_ok, comb_t_ok_a, pick_ok, comb_b, first_w, w_hi, w_lo, wd_hi, wd_lo,
         gate_ps, up_ps, silu_ok, silc_ok, inner_ok, inner_hi, inner_lo, down, y_end, out_ok, dve_chain, xb_ok) = (
            sem(n) for n in (
                "mask_in x_in wq_in wk_in wv_in col_in gate_in w_in bo_in first_keys_in keys_t_in keys_n_in "
                "out_sent consts zero_ok mask_conv key_cols count_ps bounds_ok pool_w pool_k norm_var norm_rstd "
                "norm_x tr_ps xt_hi xt_lo q_ps q_hi q_lo acc_zero key_ps key_kept k_hi k_lo score_ps score_kept "
                "max_run max_tr max_cols max_diag_a max_diag_v max_ps max_ok max_ok_a old_diff alpha_ok shifted "
                "shifted_pool prob prob_hi prob_lo v_hi v_ok pv attn_end diag_ok sum_ok bv_ok bvo_ps bvo_ok inv_ok "
                "o_hi o_lo val_ps val_hi val_lo attn_ps x1_ok x1_tr_ps x1_t_ok gate_ok logit_ps logit_exp logit_sub "
                "comb_ok comb_ps comb_t_ok comb_t_ok_a pick_ok comb_b first_w w_hi w_lo wd_hi wd_lo gate_ps up_ps "
                "silu_ok silc_ok inner_ok inner_hi inner_lo down y_end out_ok dve_chain xb_ok").split())

        def half(t, h):
            return t[:, h * HALF:(h + 1) * HALF]

        def tile(t, i):
            return t[:, i * P:(i + 1) * P]

        def f(ap):
            return ap.bitcast(F32)

        def load_bounds(eng):
            eng.wait_ge(bounds_ok, 1)
            first = eng.value_load(bounds[0:1, 0:1], min_val=0, max_val=NC - 1)
            end = eng.value_load(bounds[0:1, 1:2], min_val=1, max_val=NC)
            blocks = eng.value_load(bounds[0:1, 2:3], min_val=1, max_val=-(-NC // BLOCK))
            chunks = eng.value_load(bounds[0:1, 3:4], min_val=1, max_val=NC)
            return first, end, blocks, chunks

        def least(eng, a, b, low, high):
            smaller = eng.alloc_register()
            register = eng.alloc_register()
            eng.reg_alu(smaller, a, b, ALU.min)
            eng.reg_alu(register, smaller, low, ALU.max)
            return eng.snap(register, min_val=low, max_val=high)

        def bounded(eng, value, low, high):
            register = eng.alloc_register()
            eng.reg_alu(register, value, 0, ALU.add)
            return eng.snap(register, min_val=low, max_val=high)

        def block_range(eng, first, end, b):
            start = bounded(eng, first + b * BLOCK, 0, NC - 1)
            size = least(eng, end - start, BLOCK, 1, BLOCK)
            return start, size, bounded(eng, b * BLOCK + size, 1, NC)

        def chunk_range(eng, b, start, i):
            return (bounded(eng, start + i, 0, NC - 1),
                    bounded(eng, b * BLOCK + i, 0, NC - 1))

        def kept(i, t, h):
            at = i * (2 * TOKENS) + (t * TOKENS + h * HALF)
            return scores[:, :, :].rearrange("p a b -> p (a b)")[:, bass.ds(at, HALF)]

        SHIFTS = (0, 1, 2)
        UNITS = [(t, h) for t in range(2) for h in range(2)]

        block = ctx.enter_context(nc.Block())

        @block.sync
        def _(sp):
            sp.dma_start(mask_u[:, :].bitcast(mybir.dt.uint32), mask).then_inc(mask_in, 16)
            sp.dma_start(x_n[:, :, :], x.rearrange("(t p) d -> p t d", p=P)).then_inc(x_in, 16)
            sp.dma_start(wk[:, :], Wk).then_inc(wk_in, 16)
            first, end, blocks, chunks = load_bounds(sp)
            sp.dma_start(keys_t[:, bass.ds(first * CHUNK, CHUNK)],
                         ctx_t[:, bass.ds(first * CHUNK, CHUNK)]).then_inc(first_keys_in, 16)
            with sp.Fori(first + 1, end) as j:
                sp.dma_start(keys_t[:, bass.ds(j * CHUNK, CHUNK)],
                             ctx_t[:, bass.ds(j * CHUNK, CHUNK)]).then_inc(keys_t_in, 16)
            with sp.Fori(first, end) as j:
                sp.dma_start(keys_n[:, bass.ds(j * 2, 2), :],
                             ctx_n[:, bass.ds(j * 2, 2), :]).then_inc(keys_n_in, 16)
            sp.dma_start(w_f[:, :, 0:4 * P], w13_t).then_inc(w_in, 16)
            sp.dma_start(w_f[:, :, 4 * P:6 * P], w2_t).then_inc(w_in, 16)
            for h in range(2):
                sp.wait_ge(out_ok, h + 1)
                sp.dma_start(half(out_t, h), half(out_s, h)).then_inc(out_sent, 16)
            sp.wait_ge(out_sent, 32)

        @block.gpsimd
        def _(pool):
            g = nc.gpsimd
            g.memset(zeros_b[:, :], 0.0).then_inc(zero_ok, 1)
            g.memset(zero_col[:, :], 0.0).then_inc(zero_ok, 1)
            g.memset(ident[:, :], 0.0).then_inc(pool_k, 1)
            g.memset(ones_f[:, :], 1.0).then_inc(consts, 1)
            pool.wait_ge(pool_k, 1)
            g.affine_select(out=ident[:, :], in_=ident[:, :], compare_op=ALU.not_equal, fill=1.0, base=0,
                            pattern=[[-1, P]], channel_multiplier=1).then_inc(consts, 1)
            g.iota(chunk_no[:, 0, :], pattern=[[1, NC]], base=1, channel_multiplier=0,
                   allow_small_or_imprecise_dtypes=True).then_inc(consts, 1)
            g.iota(chunk_no[:, 1, :], pattern=[[-1, NC]], base=NC, channel_multiplier=0,
                   allow_small_or_imprecise_dtypes=True).then_inc(consts, 1)
            g.memset(neg_half[:, :], -0.5).then_inc(consts, 1)
            pool.wait_ge(mask_conv, 3)
            g.affine_select(out=key_bias[:, :], in_=key_bias0[:, :], compare_op=ALU.is_ge, fill=PADDED,
                            base=-PAD, pattern=[[P, KT]], channel_multiplier=1).then_inc(key_cols, 1)
            pool.wait_ge(wq_in, 16)
            g.tensor_copy(wq_p[0][:, :], wq).then_inc(pool_w, 1)
            pool.wait_ge(pool_w, 1)
            g.tensor_tensor(wq_p[1][:, :], wq, f(wq_p[0][:, :]), ALU.subtract).then_inc(pool_w, 1)
            pool.wait_ge(consts, 5)
            for h in range(2):
                pool.wait_ge(norm_var, h + 1)
                g.tensor_tensor(rstd[:, h * HT:(h + 1) * HT], var[:, h * HT:(h + 1) * HT],
                                neg_half[:, 0:HT], ALU.pow).then_inc(norm_rstd, 1)
            first, end, blocks, chunks = load_bounds(pool)
            g.tensor_copy(ones_r[:, :], ones_f[:, :]).then_inc(consts, 1)
            pool.wait_ge(wv_in, 32)
            for n, (w, p) in enumerate(((wv, wv_p), (wo, wo_p))):
                g.tensor_copy(p[0][:, :], w[:, :]).then_inc(pool_w, 1)
                pool.wait_ge(pool_w, 3 + 2 * n)
                g.tensor_tensor(p[1][:, :], w[:, :], f(p[0][:, :]), ALU.subtract).then_inc(pool_w, 1)
            def key_parts(c, t):
                pool.wait_ge(key_kept, c + 1)
                pool.wait_ge(score_ps, c * 4 + (2 * t + 2))
                g.tensor_tensor(k_p[0][:, t, :], tile(k_s, t), zero_col[:, 0:1].to_broadcast([P, P]),
                                ALU.add).then_inc(k_hi, 1)
                pool.wait_ge(k_hi, c * 2 + (t + 1))
                g.tensor_tensor(k_p[1][:, t, :], tile(k_s, t), f(k_p[0][:, t, :]), ALU.subtract).then_inc(k_lo, 1)

            pool.wait_ge(zero_ok, 2)
            for t in range(2):
                key_parts(0, t)

            with pool.Fori(0, blocks) as b:
                start, size, done = block_range(pool, first, end, b)
                with pool.Fori(0, size) as i:
                    j, c = chunk_range(pool, b, start, i)
                    for t in range(2):
                        key_parts(c + 1, t)

                def shift_last(i):
                    pool.wait_ge(max_ok_a, b + 1)
                    at = kept(bounded(pool, i, 0, BLOCK - 1), 1, 1)
                    g.tensor_tensor(at, at, half(max_b, 1), ALU.subtract).then_inc(shifted_pool, 1)

                def context_parts(j, c, t):
                    pool.wait_ge(pv, c * 4 + (2 * t + 2))
                    g.tensor_copy(v_p[0][:, t, :], keys_n[:, bass.ds(j * 2 + t, 1), :].rearrange(
                        "p a d -> p (a d)")).then_inc(v_hi, 1)
                    pool.wait_ge(v_hi, c * 2 + (1 + t))
                    at = bounded(pool, j * 2 + t, 0, KT - 1)
                    g.tensor_tensor(v_p[1][:, t, :], keys_n[:, bass.ds(at, 1), :].rearrange(
                        "p a d -> p (a d)"), f(v_p[0][:, t, :]), ALU.subtract).then_inc(v_ok, 1)

                shift_last(0)
                with pool.Fori(0, size - 1) as i:
                    j, c = chunk_range(pool, b, start, i)
                    pool.wait_ge(keys_n_in, chunks * 16)
                    context_parts(j, c, 0)
                    shift_last(i + 1)
                    context_parts(j, c, 1)
                pool.wait_ge(keys_n_in, chunks * 16)
                j, c = chunk_range(pool, b, start, size - 1)
                for t in range(2):
                    context_parts(j, c, t)

            pool.wait_ge(col_in, 48)
            g.tensor_tensor(bv_mat, ones_f[:, :], bv_c[:, 0:1].to_broadcast([P, P]), ALU.mult).then_inc(bv_ok, 1)
            pool.wait_ge(gate_in, 16)
            g.tensor_copy(gate_p[0][:, :], gate[:, :]).then_inc(gate_ok, 1)
            pool.wait_ge(gate_ok, 1)
            g.tensor_tensor(gate_p[1][:, :], gate[:, :], f(gate_p[0][:, :]), ALU.subtract).then_inc(gate_ok, 1)
            g.memset(earlier[:, :, :], 1.0).then_inc(pool_k, 1)
            g.memset(row_mask[:, :], 0.0).then_inc(pool_k, 1)
            pool.wait_ge(pool_k, 3)
            g.affine_select(out=earlier[:, :, :], in_=earlier[:, :, :], compare_op=ALU.is_gt, fill=0.0, base=0,
                            pattern=[[1, E], [-1, E]], channel_multiplier=0).then_inc(consts, 1)
            for n, base in enumerate((0, -E)):
                g.affine_select(out=row_mask[:, :], in_=row_mask[:, :], compare_op=ALU.not_equal, fill=1.0,
                                base=base, pattern=[[-1, E]], channel_multiplier=1).then_inc(consts, 1)
                pool.wait_ge(consts, 8 + n)

            pool.wait_ge(w_in, 32)
            g.tensor_copy(w_p[0][0][:, :], w_f[:, 0, :]).then_inc(first_w, 1)
            pool.wait_ge(first_w, 1)
            g.tensor_tensor(w_p[0][1][:, 0:4 * P], w_f[:, 0, 0:4 * P], f(w_p[0][0][:, 0:4 * P]),
                            ALU.subtract).then_inc(w_lo, 1)
            g.tensor_tensor(w_p[0][1][:, 4 * P:6 * P], w_f[:, 0, 4 * P:6 * P], f(w_p[0][0][:, 4 * P:6 * P]),
                            ALU.subtract).then_inc(wd_lo, 1)
            pool.wait_ge(norm_x, NT)
            pool.wait_ge(bvo_ok, 1)
            for i in range(NT):
                g.tensor_tensor(x_n[:, i, :], x_n[:, i, :], bo_row[:, :], ALU.add).then_inc(xb_ok, 1)
            for h in range(2):
                pool.wait_ge(norm_var, h + 3)
                g.tensor_tensor(rstd[:, h * HT:(h + 1) * HT], var[:, h * HT:(h + 1) * HT],
                                neg_half[:, 0:HT], ALU.pow).then_inc(norm_rstd, 1)

            pool.sem_inc(inner_lo, 4)
            with pool.Fori(0, E // 2) as ep:
                for u in range(8):
                    n = ep * 8 + u
                    s = u % 4
                    pool.wait_ge(inner_hi, n + 1)
                    g.tensor_tensor(p_p[1][:, s, :], inner[:, s, :], f(p_p[0][:, s, :]),
                                    ALU.subtract).then_inc(inner_lo, 1)
                    if s == 3:
                        q = 1 - u // 4
                        pool.wait_ge(wd_hi, ep * 2 + (u // 4 + 1))
                        nxt = least(pool, ep * 2 + (1 + u // 4), E - 1, 1, E - 1)
                        g.tensor_tensor(w_p[q][1][:, 4 * P:6 * P],
                                        w_f[:, bass.ds(nxt, 1), 4 * P:6 * P].rearrange("p a d -> p (a d)"),
                                        f(w_p[q][0][:, 4 * P:6 * P]), ALU.subtract).then_inc(wd_lo, 1)

        @block.scalar
        def _(act):
            s = nc.scalar
            act.dma_start(wq, Wq).then_inc(wq_in, 16)
            for t, src in ((bq_c, bq), (bk_c, bk), (bv_c, bv)):
                act.dma_start(t[:, :], src).then_inc(col_in, 16)
            act.dma_start(bo_row[:, :], bo.to_broadcast([P, P])).then_inc(bo_in, 16)
            act.dma_start(wv[:, :], Wv).then_inc(wv_in, 16)
            act.dma_start(wo[:, :], Wo).then_inc(wv_in, 16)
            act.dma_start(gate[:, :], gate_t).then_inc(gate_in, 16)

            first, end, blocks, chunks = load_bounds(act)
            for h in range(2):
                act.wait_ge(tr_ps, h + 1)
                s.activation(half(xt_p[0], h), bank[4 + h][:, :], ACT.Copy).then_inc(xt_hi, 1)
            act.wait_ge(col_in, 48)
            act.wait_ge(key_ps, 1)
            s.activation(k_s[:, :], bank[KEY_BANK][:, 0:CHUNK], ACT.Identity, bias=bk_c[:, :]).then_inc(key_kept, 1)
            for h in range(2):
                act.wait_ge(q_ps, h + 1)
                s.activation(half(q_p[0], h), bank[h][:, :], ACT.Identity, bias=bq_c[:, :]).then_inc(q_hi, 1)
            act.wait_ge(key_cols, 1)
            act.sem_inc(score_kept, 4)
            act.sem_inc(alpha_ok, 2)

            with act.Fori(0, blocks) as b:
                start, size, done = block_range(act, first, end, b)
                with act.Fori(0, size) as i:
                    j, c = chunk_range(act, b, start, i)
                    for u, (t, h) in enumerate(UNITS):
                        if u == 1:
                            act.wait_ge(key_ps, c + 2)
                            act.wait_ge(k_lo, c * 2 + 2)
                            s.activation(k_s[:, :], bank[KEY_BANK][:, 0:CHUNK], ACT.Identity,
                                         bias=bk_c[:, :]).then_inc(key_kept, 1)
                        act.wait_ge(score_ps, c * 4 + (u + 5))
                        s.activation(kept(i, t, h), bank[SCORE_BANK[u]][:, :], ACT.Identity,
                                     bias=key_bias[:, bass.ds(j * 2 + t, 1)],
                                     scale=key_scale[:, bass.ds(j * 2 + t, 1)]).then_inc(score_kept, 1)
                act.wait_ge(max_cols, b * 2 + 1)
                for m in range(HT):
                    last = s.activation(max_mat[:, m, :], ident[:, :], ACT.Copy, scale=max_col[:, m:m + 1])
                last.then_inc(max_diag_a, 1)
                with act.If(b > 0):
                    for h in range(2):
                        act.wait_ge(old_diff, b * 2 + (h + 1))
                        s.activation(half(alpha, h), half(alpha, h), ACT.Exp).then_inc(alpha_ok, 1)
                act.wait_ge(old_diff, b * 2 + 2)
                act.wait_ge(max_ps, b * 2 + 2)
                s.activation(half(max_b, 1), bank[7][:, :], ACT.Copy).then_inc(max_ok_a, 1)
                with act.Fori(0, size) as i:
                    j, c = chunk_range(act, b, start, i)

                    def prob_high(u):
                        act.wait_ge(prob, c * 4 + (u + 1))
                        act.wait_ge(pv, c * 4 + (u + 1))
                        s.activation(p_p[0][:, u, :], bank[4 + u][:, :], ACT.Copy).then_inc(prob_hi, 1)

                    for u, (t, h) in enumerate(UNITS):
                        act.wait_ge(prob_lo, c * 4 + (u + 1))
                        if u < 3:
                            act.wait_ge(shifted, c * 3 + (u + 1))
                        else:
                            act.wait_ge(shifted_pool, c + 1)
                        s.activation(bank[4 + u][:, :], kept(i, t, h), ACT.Exp).then_inc(prob, 1)
                        if u > 0:
                            prob_high(u - 1)
                    prob_high(3)

            act.wait_ge(attn_end, 1)
            for h in range(2):
                s.activation(half(xt_p[0], h), bank[h][:, :], ACT.Copy).then_inc(o_hi, 1)
            for h in range(2):
                act.wait_ge(val_ps, h + 1)
                s.activation(half(q_p[0], h), bank[4 + h][:, :], ACT.Copy).then_inc(val_hi, 1)
            for h in range(2):
                act.wait_ge(tr_ps, h + 3)
                s.activation(half(xt_p[0], h), bank[4 + h][:, :], ACT.Copy).then_inc(xt_hi, 1)
                act.wait_ge(x1_tr_ps, h + 1)
                s.activation(half(x1_t, h), bank[6 + h][:, :], ACT.Copy).then_inc(x1_t_ok, 1)
            act.wait_ge(logit_sub, 1)
            s.activation(r8[1], r8[0], ACT.Exp).then_inc(logit_exp, 1)

            s.activation(warm[:, :], neg_half[0:1, 0:1], ACT.Silu)

            act.wait_ge(comb_ps, 2)
            s.activation(half(comb_rows, 1), bank[3][0:2 * E, :], ACT.Copy).then_inc(comb_t_ok_a, 1)

            def weights_hi(ep, u, first_tile, end_tile, done):
                q = 1 - u // 4
                nxt = least(act, ep * 2 + (1 + u // 4), E - 1, 1, E - 1)
                s.activation(w_p[q][0][:, first_tile * P:end_tile * P],
                             w_f[:, bass.ds(nxt, 1), first_tile * P:end_tile * P].rearrange("p a d -> p (a d)"),
                             ACT.Copy).then_inc(done, 1)

            def inner_high(ep, u):
                n = ep * 8 + u
                act.wait_ge(inner_ok, n + 3)
                act.wait_ge(down, n + 1)
                s.activation(p_p[0][:, u % 4, :], inner[:, u % 4, :], ACT.Copy).then_inc(inner_hi, 1)

            with act.Fori(0, E // 2) as ep:
                for u in range(8):
                    n = ep * 8 + u
                    act.wait_ge(gate_ps, n + 1)
                    act.wait_ge(silc_ok, n + 1)
                    s.activation(silu[:, u % 2, :], bank[4 + 2 * (u % 2)][:, :], ACT.Silu).then_inc(silu_ok, 1)
                    if u > 0:
                        inner_high(ep, u - 1)
                    if u % 4 == 1:
                        act.wait_ge(up_ps, n)
                        weights_hi(ep, u, 0, 4, w_hi)
                    if u % 4 == 3:
                        act.wait_ge(down, ep * 8 + (u // 4 * 4 + 4))
                        weights_hi(ep, u, 4, 6, wd_hi)
                inner_high(ep, 7)

        @block.vector
        def _(dve):
            v = nc.vector
            chain = Chain(dve, dve_chain)
            dve.wait_ge(mask_in, 16)
            v.tensor_copy(mask_f[:, :], mask_u[:, :]).then_inc(mask_conv, 1)
            dve.wait_ge(mask_conv, 1)
            v.tensor_scalar(key_scale[:, :], mask_f[:, :], SCALE, None, ALU.mult).then_inc(mask_conv, 1)
            v.tensor_scalar(key_bias0[:, :], mask_f[:, :], 1.0, -MASKED, ALU.subtract, ALU.mult).then_inc(mask_conv, 1)

            def norm_stats(src, i0, i1):
                for i in range(i0, i1):
                    chain.link(v.bn_stats(stats[:, i, :], src[:, i, :]))
                chain.settle()
                for i in range(i0, i1):
                    chain.link(v.bn_aggr(mv[:, i, :], stats[:, i, :]))
                chain.settle()
                v.tensor_scalar(var[:, i0:i1], mv[:, i0:i1, 1], EPS, None, ALU.add).then_inc(norm_var, 1)

            def norm_apply(src, i0, i1):
                for i in range(i0, i1):
                    v.tensor_scalar(xn[:, i, :], src[:, i, :], mv[:, i, 0:1], rstd[:, i:i + 1],
                                    ALU.subtract, ALU.mult).then_inc(norm_x, 1)

            dve.wait_ge(count_ps, 1)
            dve.wait_ge(consts, 4)
            chain.step(v.tensor_reduce(count[:, :], bank[6][0:1, 0:KT].rearrange("p (c t) -> p c t", t=2),
                                       X, ALU.add))
            chain.step(v.tensor_scalar(count[:, :], count[:, :], 0.0, None, ALU.is_gt))
            for i in range(2):
                chain.link(v.tensor_tensor(marked[:, i, :], count[:, :], chunk_no[:, i, :], ALU.mult))
            chain.settle()
            chain.step(v.tensor_reduce(edge[:, :], marked[:, :, :], X, ALU.max))
            chain.step(v.tensor_scalar(none[:, :], edge[:, :], 0.0, float(NC), ALU.is_equal, ALU.mult))
            chain.step(v.tensor_tensor(edge2[:, :], edge[:, :], none[:, :], ALU.add))
            chain.link(v.tensor_scalar(span[:, 0:1], edge2[:, 1:2], -1.0, float(NC), ALU.mult, ALU.add))
            chain.link(v.tensor_copy(span[:, 1:2], edge2[:, 0:1]))
            chain.settle()
            chain.step(v.tensor_tensor(span[:, 3:4], span[:, 1:2], span[:, 0:1], ALU.subtract))
            for i in range(3):
                chain.link(v.tensor_scalar(over[:, i:i + 1], span[:, 3:4], float(BLOCK * (i + 1)), None, ALU.is_gt))
            chain.settle()
            chain.step(v.tensor_reduce(span[:, 2:3], over[:, :], X, ALU.add))
            chain.step(v.tensor_scalar(span[:, 2:3], span[:, 2:3], 1.0, None, ALU.add))
            v.tensor_copy(bounds[:, :], span[:, :]).then_inc(bounds_ok, 1)

            dve.wait_ge(x_in, 16)
            for h in range(2):
                norm_stats(x_n, h * HT, (h + 1) * HT)
            for h in range(2):
                dve.wait_ge(norm_rstd, h + 1)
                norm_apply(x_n, h * HT, (h + 1) * HT)
            for h in range(2):
                dve.wait_ge(xt_hi, h + 1)
                v.tensor_tensor(half(xt_p[1], h), bank[4 + h][:, :], f(half(xt_p[0], h)),
                                ALU.subtract).then_inc(xt_lo, 1)
            for h in range(2):
                v.memset(half(run_max, h), LOWEST).then_inc(max_run, 1)
            first, end, blocks, chunks = load_bounds(dve)
            for h in range(2):
                dve.wait_ge(q_hi, h + 1)
                v.scalar_tensor_tensor(half(q_p[1], h), bank[h][:, :], bq_c[:, :], f(half(q_p[0], h)),
                                       ALU.add, ALU.subtract).then_inc(q_lo, 1)

            dve.wait_ge(acc_zero, 1)
            dve.sem_inc(prob_lo, 4)
            dve.sem_inc(old_diff, 2)
            with dve.Fori(0, blocks) as b:
                start, size, done = block_range(dve, first, end, b)
                with dve.Fori(0, size) as i:
                    j, c = chunk_range(dve, b, start, i)
                    for u, (t, h) in enumerate(UNITS):
                        dve.wait_ge(score_kept, c * 4 + (u + 5))
                        dve.wait_ge(max_run, c * 4 + (u + 1))
                        v.tensor_tensor(half(run_max, h), half(run_max, h), kept(i, t, h),
                                        ALU.max).then_inc(max_run, 1)
                for h in range(2):
                    dve.wait_ge(max_tr, b * 2 + (h + 1))
                    v.tensor_reduce(max_col[:, h * HT:(h + 1) * HT],
                                    bank[4 + h][:, :].rearrange("p (i k) -> p i k", k=P), X, ALU.max)\
                        .then_inc(max_cols, 1)
                dve.wait_ge(max_cols, b * 2 + 2)
                for m in range(HT, NT):
                    last = v.tensor_scalar(max_mat[:, m, :], ident[:, :], max_col[:, m:m + 1], None, ALU.mult)
                last.then_inc(max_diag_v, 1)
                with dve.If(b > 0):
                    for h in range(2):
                        dve.wait_ge(max_ps, b * 2 + (h + 1))
                        v.tensor_tensor(half(alpha, h), half(max_b, h), bank[6 + h][:, :],
                                        ALU.subtract).then_inc(old_diff, 1)
                    for h in range(2):
                        dve.wait_ge(alpha_ok, b * 2 + (h + 1))
                        for acc in (h, 2 + h):
                            v.tensor_tensor(bank[acc][:, :], bank[acc][:, :], half(alpha, h), ALU.mult)\
                                .then_inc(acc_zero, 1)

                def low(n, u):
                    dve.wait_ge(prob_hi, n)
                    v.tensor_tensor(p_p[1][:, u, :], bank[4 + u][:, :], f(p_p[0][:, u, :]),
                                    ALU.subtract).then_inc(prob_lo, 1)

                def shift(i, u):
                    t, h = UNITS[u]
                    at = kept(i, t, h)
                    v.tensor_tensor(at, at, half(max_b, h), ALU.subtract).then_inc(shifted, 1)

                dve.wait_ge(max_ps, b * 2 + 1)
                v.tensor_copy(half(max_b, 0), bank[6][:, :]).then_inc(max_ok, 1)
                for u in SHIFTS:
                    if u == 0:
                        dve.wait_ge(max_ok, b + 1)
                    if u == 1:
                        dve.wait_ge(max_ok_a, b + 1)
                    shift(0, u)
                with dve.Fori(0, size - 1) as i:
                    j, c = chunk_range(dve, b, start, i)
                    for u in range(4):
                        low(c * 4 + (u + 1), u)
                        if u < 3:
                            shift(i + 1, SHIFTS[u])
                j, c = chunk_range(dve, b, start, size - 1)
                for u in range(4):
                    low(c * 4 + (u + 1), u)

            dve.wait_ge(attn_end, 1)
            for h in range(2):
                dve.wait_ge(o_hi, h + 1)
                v.tensor_tensor(half(xt_p[1], h), bank[h][:, :], f(half(xt_p[0], h)), ALU.subtract).then_inc(o_lo, 1)
            for h in range(2):
                v.tensor_tensor(sum_diag[:, h * HT:(h + 1) * HT, :],
                                bank[2 + h][:, :].rearrange("p (i k) -> p i k", k=P),
                                ident[:, :].unsqueeze(1).to_broadcast([P, HT, P]), ALU.mult).then_inc(diag_ok, 1)
            dve.wait_ge(bo_in, 16)
            dve.wait_ge(bvo_ps, 1)
            v.tensor_tensor(bo_row[:, :], bo_row[:, :], bank[7][:, 0:P], ALU.add).then_inc(bvo_ok, 1)
            for h in range(2):
                dve.wait_ge(val_hi, h + 1)
                v.tensor_tensor(half(q_p[1], h), bank[4 + h][:, :], f(half(q_p[0], h)),
                                ALU.subtract).then_inc(val_lo, 1)
            dve.wait_ge(diag_ok, 2)
            v.tensor_reduce(sum_col, sum_diag, X, ALU.add).then_inc(sum_ok, 1)
            dve.wait_ge(sum_ok, 1)
            v.reciprocal(inv_sum[:, :], sum_col).then_inc(inv_ok, 1)
            dve.wait_ge(inv_ok, 1)
            for h in range(2):
                dve.wait_ge(attn_ps, h + 1)
                dve.wait_ge(xb_ok, (h + 1) * HT)
                for i in range(HT):
                    t = h * HT + i
                    v.scalar_tensor_tensor(x1[:, t, :], bank[6 + h][:, i * P:(i + 1) * P], inv_sum[:, t:t + 1],
                                           x_n[:, t, :], ALU.mult, ALU.add).then_inc(x1_ok, 1)
                dve.wait_ge(x1_ok, (h + 1) * HT)
                norm_stats(x1, h * HT, (h + 1) * HT)
            for h in range(2):
                dve.wait_ge(norm_rstd, h + 3)
                norm_apply(x1, h * HT, (h + 1) * HT)
            for h in range(2):
                dve.wait_ge(xt_hi, h + 3)
                v.tensor_tensor(half(xt_p[1], h), bank[4 + h][:, :], f(half(xt_p[0], h)),
                                ALU.subtract).then_inc(xt_lo, 1)

            dve.wait_ge(logit_ps, 1)
            logits = bank[2][:, 0:NT * E].rearrange("p (t e) -> p t e", e=E)
            chain.step(v.tensor_reduce(r1[0], logits, X, ALU.max))
            v.tensor_tensor(r8[0], logits, r1[0].unsqueeze(2).to_broadcast([P, NT, E]),
                            ALU.subtract).then_inc(logit_sub, 1)
            dve.wait_ge(logit_exp, 1)
            chain.step(v.tensor_reduce(r1[1], r8[1], X, ALU.add))
            chain.step(v.reciprocal(r1[2], r1[1]))
            chain.step(v.tensor_tensor(r8[2], r8[1], r1[2].unsqueeze(2).to_broadcast(
                [P, NT, E]), ALU.mult))
            chain.step(v.tensor_reduce(g4[0], r8[2].rearrange("p t (g k) -> p t g k", k=EG),
                                       X, ALU.max))

            def keep_top(keep, val, n):
                first_i = pair[0][:, :, 0:n, 0:n]
                second = pair[1][:, :, 0:n, 0:n]
                mine = val.unsqueeze(3).to_broadcast([P, NT, n, n])
                other = val.unsqueeze(2).to_broadcast([P, NT, n, n])
                chain.link(v.tensor_tensor(first_i, other, mine, ALU.is_equal))
                chain.link(v.tensor_tensor(second, other, mine, ALU.is_gt))
                chain.settle()
                chain.step(v.tensor_tensor(first_i, first_i, earlier[:, 0:n, 0:n].unsqueeze(1).to_broadcast(
                    [P, NT, n, n]), ALU.mult))
                chain.step(v.tensor_tensor(first_i, first_i, second, ALU.add))
                chain.step(v.tensor_reduce(keep, first_i, X, ALU.add))
                chain.step(v.tensor_scalar(keep, keep, float(TOP), None, ALU.is_lt))

            keep_top(g4[1], g4[0], G)
            for k in range(EG):
                chain.link(v.tensor_tensor(r8[3].rearrange("p t (g k) -> p t g k", k=EG)[:, :, :, k],
                                           r8[2].rearrange("p t (g k) -> p t g k", k=EG)[:, :, :, k],
                                           g4[1], ALU.mult))
            chain.settle()
            keep_top(r8[4], r8[3], E)
            chain.step(v.tensor_tensor(r8[5], r8[3], r8[4], ALU.mult))
            chain.step(v.tensor_reduce(r1[0], r8[5], X, ALU.add))
            chain.step(v.reciprocal(r1[1], r1[0]))
            chain.step(v.tensor_tensor(r8[6], r8[5], r1[1].unsqueeze(2).to_broadcast(
                [P, NT, E]), ALU.mult))
            hi = r8[7].bitcast(F32R)
            chain.step(v.tensor_copy(hi, r8[6]))
            v.tensor_copy(comb[:, :, 0:E], r8[7]).then_inc(comb_ok, 1)
            v.tensor_tensor(comb[:, :, E:2 * E], r8[6], r8[7], ALU.subtract).then_inc(comb_ok, 1)
            dve.wait_ge(comb_ps, 1)
            v.tensor_copy(half(comb_rows, 0), bank[2][0:2 * E, :]).then_inc(comb_t_ok, 1)
            v.tensor_scalar(pick[0][:, :], ones_f[0:2 * E, :], row_mask[:, 0:1], None, ALU.mult).then_inc(pick_ok, 1)
            dve.sem_inc(silc_ok, 2)
            dve.sem_inc(inner_ok, 2)
            with dve.Fori(0, E // 2) as ep:
                for u in range(8):
                    n = ep * 8 + u
                    h = (u // 2) % 2
                    if u % 4 == 0:
                        q = 1 - u // 4
                        nxt = least(dve, ep * 2 + (1 + u // 4), E - 1, 1, E - 1)
                        v.tensor_scalar(pick[q][:, :], ones_f[0:2 * E, :], row_mask[:, bass.ds(nxt, 1)], None,
                                        ALU.mult).then_inc(pick_ok, 1)
                    dve.wait_ge(silu_ok, n + 1)
                    dve.wait_ge(comb_b, ep * 4 + (u // 2 + 1))
                    v.tensor_tensor(silc[:, u % 2, :], silu[:, u % 2, :], bank[2 + h][:, :],
                                    ALU.mult).then_inc(silc_ok, 1)
                    dve.wait_ge(up_ps, n + 1)
                    dve.wait_ge(silc_ok, n + 3)
                    dve.wait_ge(inner_lo, n + 1)
                    v.tensor_tensor(inner[:, u % 4, :], silc[:, u % 2, :], bank[5 + 2 * (u % 2)][:, :],
                                    ALU.mult).then_inc(inner_ok, 1)
                    if u % 4 == 2:
                        q = 1 - u // 4
                        nxt = least(dve, ep * 2 + (1 + u // 4), E - 1, 1, E - 1)
                        dve.wait_ge(w_hi, ep * 2 + (1 + u // 4))
                        v.tensor_tensor(w_p[q][1][:, 0:4 * P],
                                        w_f[:, bass.ds(nxt, 1), 0:4 * P].rearrange("p a d -> p (a d)"),
                                        f(w_p[q][0][:, 0:4 * P]), ALU.subtract).then_inc(w_lo, 1)
            dve.wait_ge(x1_t_ok, 2)
            for h in range(2):
                dve.wait_ge(y_end, h + 1)
                v.tensor_tensor(half(out_s, h), bank[h][:, :], half(x1_t, h), ALU.add).then_inc(out_ok, 1)

        @block.tensor
        def _(pe):
            mm = nc.tensor.matmul

            def product(out, lhs, rhs, start=True, stop=True):
                grouped = dict(skip_group_check=not (start and stop))
                mm(out, lhs[0], rhs[0], start=start, stop=False, **grouped)
                mm(out, lhs[1], rhs[0], start=False, stop=False, **grouped)
                return mm(out, lhs[0], rhs[1], start=False, stop=stop, **grouped)

            def halves(t, h):
                return tuple(half(x_, h) for x_ in t)

            def keep_clock(products, banks, start=False):
                for n in range(products):
                    mm(bank[banks[n % len(banks)]][:, :], zeros_b[:, :], zeros_b[:, 0:1].to_broadcast([P, HALF]),
                       start=start and n < len(banks), stop=False, skip_group_check=True)

            pe.wait_ge(consts, 1)
            pe.wait_ge(mask_conv, 1)
            mm(bank[6][0:1, 0:KT], ones_f[:, 0:1], mask_f[:, :], start=True, stop=True).then_inc(count_ps, 1)
            pe.wait_ge(zero_ok, 1)
            first, end, blocks, chunks = load_bounds(pe)
            pe.wait_ge(consts, 2)
            for h in range(2):
                for i in range(HT):
                    pe.wait_ge(norm_x, h * HT + i + 1)
                    last = nc.tensor.transpose(bank[4 + h][:, i * P:(i + 1) * P], xn[:, h * HT + i, :], ident[:, :])
                last.then_inc(tr_ps, 1)
            pe.sem_inc(score_ps, 4)
            pe.wait_ge(wk_in, 16)
            pe.wait_ge(first_keys_in, 16)
            mm(bank[KEY_BANK][:, 0:CHUNK], wk[:, :], keys_t[:, bass.ds(first * CHUNK, CHUNK)],
               start=True, stop=True).then_inc(key_ps, 1)
            pe.wait_ge(pool_w, 2)
            for h in range(2):
                pe.wait_ge(xt_lo, h + 1)
                product(bank[h][:, :], [w[:, :] for w in wq_p], halves(xt_p, h)).then_inc(q_ps, 1)

            pe.wait_ge(consts, 6)
            pe.wait_ge(q_lo, 2)
            for n in range(4):
                last = mm(bank[n][:, :], zeros_b[:, :], zeros_b[:, 0:1].to_broadcast([P, HALF]), start=True,
                          stop=False, skip_group_check=True)
            last.then_inc(acc_zero, 1)
            pe.sem_inc(keys_t_in, 16)
            pe.sem_inc(pv, 4)
            with pe.Fori(0, blocks) as b:
                start, size, done = block_range(pe, first, end, b)
                with pe.Fori(0, size) as i:
                    j, c = chunk_range(pe, b, start, i)
                    for u, (t, h) in enumerate(UNITS):
                        if u == 0:
                            pe.wait_ge(prob_lo, b * (4 * BLOCK) + 4)
                        if h == 0:
                            pe.wait_ge(k_lo, c * 2 + (t + 1))
                        if u == 1:
                            pe.wait_ge(score_kept, c * 4 + 3)
                            pe.wait_ge(key_kept, c + 1)
                            pe.wait_ge(keys_t_in, chunks * 16)
                            nxt = least(pe, j + 1, end - 1, 0, NC - 1)
                            mm(bank[KEY_BANK][:, 0:CHUNK], wk[:, :], keys_t[:, bass.ds(nxt * CHUNK, CHUNK)],
                               start=True, stop=True).then_inc(key_ps, 1)
                        pe.wait_ge(score_kept, c * 4 + (u + 1))
                        if u == 2:
                            pe.wait_ge(key_kept, c + 2)
                        product(bank[SCORE_BANK[u]][:, :], [k[:, t, :] for k in k_p],
                                halves(q_p, h)).then_inc(score_ps, 1)
                for h in range(2):
                    pe.wait_ge(max_run, done * 4 + (h + 1))
                    for i in range(HT):
                        last = nc.tensor.transpose(bank[4 + h][:, i * P:(i + 1) * P],
                                                   tile(run_max, h * HT + i), ident[:, :])
                    last.then_inc(max_tr, 1)
                keep_clock(FILL_MAXIMA, (0, 1, 2, 3))
                pe.wait_ge(key_kept, done + 1)
                for h in range(2):
                    pe.wait_ge(max_diag_v if h else max_diag_a, b + 1)
                    for i in range(HT):
                        last = mm(bank[6 + h][:, i * P:(i + 1) * P], ones_f[:, :], max_mat[:, h * HT + i, :],
                                  start=True, stop=True)
                    last.then_inc(max_ps, 1)
                pe.wait_ge(acc_zero, b * 4 + 1)
                keep_clock(FILL_SHIFT, (0, 1, 2, 3))
                with pe.Fori(0, size) as i:
                    j, c = chunk_range(pe, b, start, i)
                    for u, (t, h) in enumerate(UNITS):
                        if u == 0:
                            pe.wait_ge(acc_zero, b * 4 + 1)
                        if h == 0:
                            pe.wait_ge(v_ok, c * 2 + (t + 1))
                        pe.wait_ge(prob_lo, c * 4 + (u + 5))
                        product(bank[h][:, :], [w[:, t, :] for w in v_p], [w[:, u, :] for w in p_p],
                                start=False, stop=False)
                        for w in p_p:
                            last = mm(bank[2 + h][:, :], ones_r[:, :], w[:, u, :], start=False, stop=False,
                                      skip_group_check=True)
                        last.then_inc(pv, 1)
            for n in range(4):
                last = mm(bank[n][:, :], zeros_b[:, :], zeros_b[:, 0:1].to_broadcast([P, HALF]), start=False, stop=True,
                          skip_group_check=True)
            last.then_inc(attn_end, 1)

            pe.wait_ge(bv_ok, 1)
            pe.wait_ge(wv_in, 32)
            mm(bank[7][:, 0:P], bv_mat, wo[:, :], start=True, stop=True).then_inc(bvo_ps, 1)
            pe.wait_ge(pool_w, 6)
            for h in range(2):
                pe.wait_ge(o_lo, h + 1)
                product(bank[4 + h][:, :], [w[:, :] for w in wv_p], halves(xt_p, h)).then_inc(val_ps, 1)
            pe.wait_ge(bvo_ok, 1)
            for h in range(2):
                pe.wait_ge(val_lo, h + 1)
                for i in range(HT):
                    last = product(bank[6 + h][:, i * P:(i + 1) * P], [tile(w, h * HT + i) for w in q_p],
                                   [w[:, :] for w in wo_p])
                last.then_inc(attn_ps, 1)
            keep_clock(FILL_NORM, (0, 1), start=True)
            for h in range(2):
                for i in range(HT):
                    pe.wait_ge(norm_x, NT + h * HT + i + 1)
                    last = nc.tensor.transpose(bank[4 + h][:, i * P:(i + 1) * P], xn[:, h * HT + i, :], ident[:, :])
                last.then_inc(tr_ps, 1)
                for i in range(HT):
                    last = nc.tensor.transpose(bank[6 + h][:, i * P:(i + 1) * P], x1[:, h * HT + i, :], ident[:, :])
                last.then_inc(x1_tr_ps, 1)
            pe.wait_ge(gate_ok, 2)
            for i in range(NT):
                if i % HT == 0:
                    pe.wait_ge(xt_lo, 3 + i // HT)
                last = product(bank[2][:, i * E:(i + 1) * E], [tile(w, i) for w in xt_p], [w[:, :] for w in gate_p])
            last.then_inc(logit_ps, 1)

            def gate_up(u):
                h, it, q = (u // 2) % 2, u % 2, u // 4
                product(bank[4 + 2 * (u % 2)][:, :], [tile(w, it) for w in w_p[q]],
                        halves(xt_p, h)).then_inc(gate_ps, 1)
                product(bank[5 + 2 * (u % 2)][:, :], [tile(w, 2 + it) for w in w_p[q]],
                        halves(xt_p, h)).then_inc(up_ps, 1)

            def down_product(u, low_parts):
                h, it, q = (u // 2) % 2, u % 2, u // 4
                pe.wait_ge(inner_lo, low_parts)
                product(bank[h][:, :], [tile(w, 4 + it) for w in w_p[q]], [w[:, u % 4, :] for w in p_p],
                        start=False, stop=False).then_inc(down, 1)

            def combine(q, h, n):
                pe.wait_ge(pick_ok, n)
                mm(bank[2 + h][:, :], pick[q][:, :], half(comb_rows, h), start=True,
                   stop=True).then_inc(comb_b, 1)

            pe.wait_ge(x1_t_ok, 2)
            pe.wait_ge(w_lo, 1)
            for u in range(2):
                gate_up(u)
            keep_clock(FILL_ROUTING, (0, 1))
            pe.wait_ge(comb_ok, 2)
            for h in range(2):
                for i in range(HT):
                    last = nc.tensor.transpose(bank[2 + h][0:2 * E, i * P:(i + 1) * P], comb[:, h * HT + i, :],
                                               ident[:, :])
                last.then_inc(comb_ps, 1)
            keep_clock(FILL_COMBINE, (0, 1))
            for h in range(2):
                pe.wait_ge(comb_t_ok_a if h else comb_t_ok, 1)
                combine(0, h, 1)

            def gate_up_ahead(ep, u):
                n = ep * 8 + u
                m = (u + 2) % 8
                if m % 4 == 0:
                    pe.wait_ge(w_lo, ep * 2 + ((u + 2) // 4 + 1))
                pe.wait_ge(inner_ok, n + 3)
                gate_up(m)
                if m % 2 == 0:
                    pe.wait_ge(silc_ok, n + 4)
                    combine(((u + 4) // 4) % 2, 1 - (m // 2) % 2, ep * 2 + (1 + (u + 4) // 4))

            pe.sem_inc(down, 4)
            with pe.Fori(0, E // 2) as ep:
                for u in range(8):
                    if u < 6:
                        gate_up_ahead(ep, u)
                    else:
                        with pe.If(ep < E // 2 - 1):
                            gate_up_ahead(ep, u)
                    if u > 0:
                        if u % 4 == 1:
                            pe.wait_ge(wd_lo, ep * 2 + (u // 4 + 1))
                        down_product(u - 1, ep * 8 + (u + 4))
                    else:
                        with pe.If(ep > 0):
                            down_product(7, ep * 8 + 4)
            for h in range(2):
                if h == 1:
                    down_product(7, E * 4 + 4)
                mm(bank[h][:, :], zeros_b[:, :], zeros_b[:, 0:1].to_broadcast([P, HALF]), start=False, stop=True,
                   skip_group_check=True).then_inc(y_end, 1)


_INS = ["x", "mask", "ctx_t", "ctx_n", "Wq", "bq", "Wk", "bk", "Wv", "bv", "Wo", "bo", "gate_t", "w13_t", "w2_t"]


def kernel(**inputs):
    import numpy as np
    import concourse.bacc as bacc
    from concourse.bass_utils import run_bass_kernel_spmd

    a = {k.replace("L0_xattn_", "").replace("L0_ffn_", ""): np.asarray(v) for k, v in inputs.items()}
    context = a["ctx_1024"][0]
    keys, width = context.shape
    whole = -(-keys // CHUNK) * CHUNK
    padded = np.zeros((whole, width), context.dtype)
    padded[whole - keys:] = context
    mask = np.zeros(whole, np.uint8)
    mask[whole - keys:] = a["mask_BxS2_bk0"][0].view(np.uint8)
    experts, _, inter = a["w2_weight"].shape
    data = {
        "x": a["x"][0],
        "mask": np.ascontiguousarray(mask.reshape(-1, P).T).view(np.uint32),
        "ctx_t": padded.T,
        "ctx_n": padded.reshape(-1, P, width).transpose(1, 0, 2),
        "gate_t": a["gate_w"].T,
        "w13_t": a["w13_weight"].transpose(2, 0, 1),
        "w2_t": a["w2_weight"].reshape(experts, width, inter // P, P).transpose(3, 0, 2, 1).reshape(P, experts, -1),
    }
    for name in ("Wq", "Wk", "Wv", "Wo"):
        data[name] = a[name]
    for name in ("bq", "bk", "bv"):
        data[name] = a[name].reshape(P, 1)
    data["bo"] = a["bo"].reshape(1, P)

    nc = bacc.Bacc("TRN2", target_bir_lowering=False, num_devices=1)
    arrays, args = {}, []
    for name in _INS:
        array = np.ascontiguousarray(data[name])
        arrays[f"in_{name}"] = array
        args.append(nc.dram_tensor(f"in_{name}", array.shape, mybir.dt.from_np(array.dtype),
                                   kind="ExternalInput").ap())
    tokens = data["x"].shape[0]
    out = nc.dram_tensor("out_t", (width, tokens), F32, kind="ExternalOutput").ap()
    xattn_ffn(nc, keys, *args, out)
    result = run_bass_kernel_spmd(nc, [arrays], core_ids=[0])
    return np.ascontiguousarray(result.results[0]["out_t"].T).reshape(1, tokens, width)
```

```python
from contextlib import ExitStack

import concourse.bass as bass
from concourse import mybir

F32 = mybir.dt.float32
F32R = mybir.dt.float32r
BF16 = mybir.dt.bfloat16
I32 = mybir.dt.int32
ALU = mybir.AluOpType
ACT = mybir.ActivationFunctionType
X = mybir.AxisListType.X

P = 128
HALF = 512
CHUNK = 2 * P
MASKED = -1.0e9
PADDED = -3.0e9
LOWEST = -3.0e38
EPS = 1e-5
BLOCK = 7
FILL_VALUES, FILL_MAXIMA, FILL_SHIFT, FILL_NORM, FILL_ROUTING, FILL_COMBINE = 5, 6, 12, 14, 24, 4
SCORE_BANK = (4, 5, 6, 7)
KEY_BANK = 3
QUERY_BANK = (7, 4)


class Chain:

    def __init__(self, engine, sem):
        self.engine, self.sem, self.value = engine, sem, 0

    def link(self, instruction):
        instruction.then_inc(self.sem, 1)
        self.value += 1

    def settle(self):
        self.engine.wait_ge(self.sem, self.value)

    def step(self, instruction):
        self.link(instruction)
        self.settle()


def xattn_ffn(nc, keys, x, mask, ctx_t, ctx_n, Wq, bq, Wk, bk, Wv_t, bv, Wo, bo, gate_t, w13_t, w2_t, out_t):
    TOKENS = x.shape[0]
    NT = TOKENS // P
    HT = HALF // P
    KT = 4 * mask.shape[1]
    NC = KT // 2
    PAD = ctx_t.shape[1] - keys
    E = w13_t.shape[1]
    SCALE = float(P) ** -0.5
    EG = 2
    G = E // EG
    TOP = 2
    assert TOKENS == 2 * HALF and ctx_t.shape[1] == KT * P and PAD >= 0

    with ExitStack() as ctx:
        def sb(name, shape, dt=F32):
            return ctx.enter_context(nc.sbuf_tensor(name, shape, dt))

        def sem(name):
            return ctx.enter_context(nc.semaphore(name))

        bank = [ctx.enter_context(nc.psum_tensor(f"bank{i}", [P, HALF], F32)) for i in range(8)]

        ident = sb("ident", [P, P])
        ones_f = sb("ones_f", [P, P])
        ones_half = [sb(f"ones_half{h}", [P, P], F32R) for h in range(2)]
        zeros_b = sb("zeros_b", [P, P], BF16)
        neg_half = sb("neg_half", [P, NT])
        chunk_no = sb("chunk_no", [1, 2, NC])
        earlier = sb("earlier", [P, E, E], BF16)
        row_mask = sb("row_mask", [2 * E, E])

        x_n = sb("x_n", [P, NT, P])
        bo_row = sb("bo_row", [P, P])
        mask_u = sb("mask_u", [P, KT], mybir.dt.uint8)
        keys_t = sb("keys_t", [P, KT * P])
        keys_n = sb("keys_n", [P, KT, P])
        k_s = sb("k_s", [P, CHUNK])
        wq = k_s[:, 0:P]
        bv_mat = k_s[:, P:2 * P]
        wk, wv_t, wo = (sb(n, [P, P]) for n in ("wk", "wv_t", "wo"))
        wvo = sb("wvo", [P, P])
        bq_c, bk_c, bv_c = (sb(n, [P, 1]) for n in ("bq_c", "bk_c", "bv_c"))
        gate = sb("gate", [P, E])
        w_f = sb("w_f", [P, E, 6 * P])

        def parts(name, shape):
            return sb(name + "_hi", shape, F32R), sb(name + "_lo", shape, F32R)

        wq_p, wvo_p = parts("wq_p", [P, P]), parts("wvo_p", [P, P])
        gate_p = parts("gate_p", [P, E])
        xt_p = parts("xt_p", [P, TOKENS])
        q_p = parts("q_p", [P, TOKENS])
        zero_col = sb("zero_col", [P, 1])
        k_p = parts("k_p", [P, 2, P])
        v_p = parts("v_p", [P, 2, P])
        p_p = parts("p_p", [P, 4, HALF])
        w_p = [parts(f"w_p{i}", [P, 6 * P]) for i in range(2)]
        pick = [sb(f"pick{i}", [2 * E, P], F32R) for i in range(2)]
        warm = sb("warm", [1, 1])
        inv_sum = sb("inv_sum", [P, NT])

        stats = sb("stats", [P, NT, 6])
        mv = sb("mv", [P, NT, 2])
        var = sb("var", [P, NT])
        rstd = sb("rstd", [P, NT])
        xn = sb("xn", [P, NT, P])
        mask_f = sb("mask_f", [P, KT])
        key_scale = sb("key_scale", [P, KT])
        key_bias0 = sb("key_bias0", [P, KT])
        key_bias = sb("key_bias", [P, KT])
        count = sb("count", [1, NC])
        marked = sb("marked", [1, 2, NC])
        edge = sb("edge", [1, 2])
        none = sb("none", [1, 2])
        edge2 = sb("edge2", [1, 2])
        span = sb("span", [1, 4])
        over = sb("over", [1, 3])
        bounds = sb("bounds", [1, 4], I32)
        scores = sb("scores", [P, 2 * BLOCK, TOKENS])
        run_max = sb("run_max", [P, TOKENS])
        max_col = sb("max_col", [P, NT])
        max_mat = xn
        max_b = sb("max_b", [P, TOKENS])
        alpha = xn[:, :, :].rearrange("p a b -> p (a b)")
        late_at = [0]

        def late(*shape):
            size = 1
            for n in shape:
                size *= n
            at = late_at[0]
            late_at[0] += size
            assert late_at[0] <= 2 * BLOCK * TOKENS
            flat = scores[:, :, :].rearrange("p a b -> p (a b)")[:, at:at + size]
            if len(shape) == 1:
                return flat
            names = "abc"[:len(shape)]
            return flat.rearrange(f"p ({' '.join(names)}) -> p {' '.join(names)}",
                                  **dict(zip(names[1:], shape[1:])))

        sums = late(HALF)
        x1 = late(NT, P)
        x1_t = late(TOKENS)
        out_s = late(TOKENS)
        r8 = [late(NT, E) for i in range(7)]
        r1 = [late(NT) for i in range(3)]
        g4 = [late(NT, G) for i in range(3)]
        pair = [late(NT, E, E // 2).bitcast(BF16) for i in range(2)]
        comb = late(NT, 2 * E)
        comb_rows = q_p[0][0:2 * E, :]
        silu = late(2, HALF)
        silc = late(2, HALF)
        inner = late(4, HALF)

        (mask_in, x_in, wq_in, wk_in, wv_in, col_in, gate_in, w_in, bo_in, first_keys_in, keys_t_in, keys_n_in,
         out_sent, consts, ones_ok, zero_ok, mask_conv, key_cols, count_ps, bounds_ok, pool_w, pool_k, norm_var,
         norm_rstd, norm_x, tr_ps, xt_hi, xt_lo, q_ps, q_hi, q_lo, acc_zero, key_ps, key_kept, k_hi, k_lo, score_ps,
         score_kept, max_run, max_tr, max_cols, max_diag_a, max_diag_v, max_ps, max_ok, max_ok_a, old_diff, alpha_ok,
         shifted, shifted_pool, prob, prob_hi, prob_lo, v_hi, v_ok, pv, attn_end, row_ok, sum_ps, bv_ok, wvo_ps,
         wvo_ok, bvo_ps, bvo_ok, inv_ok, o_hi, o_lo, attn_ps, x1_ok, x1_tr_ps, x1_t_ok, gate_ok, logit_ps, logit_exp,
         logit_sub, comb_ok, comb_ps, comb_t_ok, comb_t_ok_a, pick_ok, comb_b, first_w, w_hi, w_lo, wd_hi, wd_lo,
         gate_ps, up_ps, silu_ok, silc_ok, inner_ok, inner_hi, inner_lo, down, y_end, out_ok, dve_chain, xb_ok) = (
            sem(n) for n in (
                "mask_in x_in wq_in wk_in wv_in col_in gate_in w_in bo_in first_keys_in keys_t_in keys_n_in "
                "out_sent consts ones_ok zero_ok mask_conv key_cols count_ps bounds_ok pool_w pool_k norm_var "
                "norm_rstd norm_x tr_ps xt_hi xt_lo q_ps q_hi q_lo acc_zero key_ps key_kept k_hi k_lo score_ps "
                "score_kept max_run max_tr max_cols max_diag_a max_diag_v max_ps max_ok max_ok_a old_diff alpha_ok "
                "shifted shifted_pool prob prob_hi prob_lo v_hi v_ok pv attn_end row_ok sum_ps bv_ok wvo_ps wvo_ok "
                "bvo_ps bvo_ok inv_ok o_hi o_lo attn_ps x1_ok x1_tr_ps x1_t_ok gate_ok logit_ps logit_exp logit_sub "
                "comb_ok comb_ps comb_t_ok comb_t_ok_a pick_ok comb_b first_w w_hi w_lo wd_hi wd_lo gate_ps up_ps "
                "silu_ok silc_ok inner_ok inner_hi inner_lo down y_end out_ok dve_chain xb_ok").split())

        def half(t, h):
            return t[:, h * HALF:(h + 1) * HALF]

        def side(t, h):
            return t[:, h * (P // 2):(h + 1) * (P // 2)]

        def tile(t, i):
            return t[:, i * P:(i + 1) * P]

        def f(ap):
            return ap.bitcast(F32)

        def load_bounds(eng):
            eng.wait_ge(bounds_ok, 1)
            first = eng.value_load(bounds[0:1, 0:1], min_val=0, max_val=NC - 1)
            end = eng.value_load(bounds[0:1, 1:2], min_val=1, max_val=NC)
            blocks = eng.value_load(bounds[0:1, 2:3], min_val=1, max_val=-(-NC // BLOCK))
            chunks = eng.alloc_register()
            eng.reg_alu(chunks, end - first, 1, ALU.max)
            return first, end, blocks, eng.snap(chunks, min_val=1, max_val=NC)

        def least(eng, a, b, low, high):
            smaller = eng.alloc_register()
            register = eng.alloc_register()
            eng.reg_alu(smaller, a, b, ALU.min)
            eng.reg_alu(register, smaller, low, ALU.max)
            return eng.snap(register, min_val=low, max_val=high)

        def bounded(eng, value, low, high):
            register = eng.alloc_register()
            eng.reg_alu(register, value, 0, ALU.add)
            return eng.snap(register, min_val=low, max_val=high)

        def block_range(eng, first, end, b):
            start = bounded(eng, first + b * BLOCK, 0, NC - 1)
            size = least(eng, end - start, BLOCK, 1, BLOCK)
            return start, size, bounded(eng, b * BLOCK + size, 1, NC)

        def chunk_range(eng, b, start, i):
            return (bounded(eng, start + i, 0, NC - 1),
                    bounded(eng, b * BLOCK + i, 0, NC - 1))

        def kept(i, t, h):
            at = i * (2 * TOKENS) + (t * TOKENS + h * HALF)
            return scores[:, :, :].rearrange("p a b -> p (a b)")[:, bass.ds(at, HALF)]

        SHIFTS = (0, 1, 2)
        UNITS = [(t, h) for t in range(2) for h in range(2)]

        block = ctx.enter_context(nc.Block())

        @block.sync
        def _(sp):
            sp.dma_start(mask_u[:, :].bitcast(mybir.dt.uint32), mask).then_inc(mask_in, 16)
            sp.dma_start(x_n[:, :, :], x.rearrange("(t p) d -> p t d", p=P)).then_inc(x_in, 16)
            sp.dma_start(wk[:, :], Wk).then_inc(wk_in, 16)
            first, end, blocks, chunks = load_bounds(sp)
            sp.dma_start(keys_t[:, bass.ds(first * CHUNK, CHUNK)],
                         ctx_t[:, bass.ds(first * CHUNK, CHUNK)]).then_inc(first_keys_in, 16)
            with sp.Fori(first + 1, end) as j:
                sp.dma_start(keys_t[:, bass.ds(j * CHUNK, CHUNK)],
                             ctx_t[:, bass.ds(j * CHUNK, CHUNK)]).then_inc(keys_t_in, 16)
            with sp.Fori(first, end) as j:
                sp.dma_start(keys_n[:, bass.ds(j * 2, 2), :],
                             ctx_n[:, bass.ds(j * 2, 2), :]).then_inc(keys_n_in, 16)
            sp.dma_start(w_f[:, :, 0:4 * P], w13_t).then_inc(w_in, 16)
            sp.dma_start(w_f[:, :, 4 * P:6 * P], w2_t).then_inc(w_in, 16)
            for h in range(2):
                sp.wait_ge(out_ok, h + 1)
                sp.dma_start(half(out_t, h), half(out_s, h)).then_inc(out_sent, 16)
            sp.wait_ge(out_sent, 32)

        @block.gpsimd
        def _(pool):
            g = nc.gpsimd
            g.memset(zeros_b[:, :], 0.0).then_inc(zero_ok, 1)
            g.memset(zero_col[:, :], 0.0).then_inc(zero_ok, 1)
            g.memset(ident[:, :], 0.0).then_inc(pool_k, 1)
            g.memset(ones_f[:, :], 1.0).then_inc(consts, 1)
            pool.wait_ge(pool_k, 1)
            g.affine_select(out=ident[:, :], in_=ident[:, :], compare_op=ALU.not_equal, fill=1.0, base=0,
                            pattern=[[-1, P]], channel_multiplier=1).then_inc(consts, 1)
            g.iota(chunk_no[:, 0, :], pattern=[[1, NC]], base=1, channel_multiplier=0,
                   allow_small_or_imprecise_dtypes=True).then_inc(consts, 1)
            g.iota(chunk_no[:, 1, :], pattern=[[-1, NC]], base=NC, channel_multiplier=0,
                   allow_small_or_imprecise_dtypes=True).then_inc(consts, 1)
            g.memset(neg_half[:, :], -0.5).then_inc(consts, 1)
            pool.wait_ge(mask_conv, 3)
            g.affine_select(out=key_bias[:, :], in_=key_bias0[:, :], compare_op=ALU.is_ge, fill=PADDED,
                            base=-PAD, pattern=[[P, KT]], channel_multiplier=1).then_inc(key_cols, 1)
            pool.wait_ge(wq_in, 16)
            g.tensor_copy(wq_p[0][:, :], wq).then_inc(pool_w, 1)
            pool.wait_ge(pool_w, 1)
            g.tensor_tensor(wq_p[1][:, :], wq, f(wq_p[0][:, :]), ALU.subtract).then_inc(pool_w, 1)
            pool.wait_ge(consts, 5)
            for h in range(2):
                pool.wait_ge(norm_var, h + 1)
                g.tensor_tensor(rstd[:, h * HT:(h + 1) * HT], var[:, h * HT:(h + 1) * HT],
                                neg_half[:, 0:HT], ALU.pow).then_inc(norm_rstd, 1)
            first, end, blocks, chunks = load_bounds(pool)
            for h in range(2):
                g.tensor_copy(side(ones_half[h][:, :], h), side(ones_f[:, :], h)).then_inc(ones_ok, 1)
                g.tensor_copy(side(ones_half[h][:, :], 1 - h), zero_col[:, 0:1].to_broadcast([P, P // 2]))\
                    .then_inc(ones_ok, 1)
            pool.wait_ge(wvo_ok, 1)
            g.tensor_copy(wvo_p[0][:, :], wvo[:, :]).then_inc(pool_w, 1)
            pool.wait_ge(pool_w, 3)
            g.tensor_tensor(wvo_p[1][:, :], wvo[:, :], f(wvo_p[0][:, :]), ALU.subtract).then_inc(pool_w, 1)

            def key_parts(c, t):
                pool.wait_ge(key_kept, c + 1)
                pool.wait_ge(score_ps, c * 4 + (2 * t + 2))
                g.tensor_tensor(k_p[0][:, t, :], tile(k_s, t), zero_col[:, 0:1].to_broadcast([P, P]),
                                ALU.add).then_inc(k_hi, 1)
                pool.wait_ge(k_hi, c * 2 + (t + 1))
                g.tensor_tensor(k_p[1][:, t, :], tile(k_s, t), f(k_p[0][:, t, :]), ALU.subtract).then_inc(k_lo, 1)

            pool.wait_ge(zero_ok, 2)
            for t in range(2):
                key_parts(0, t)

            with pool.Fori(0, blocks) as b:
                start, size, done = block_range(pool, first, end, b)
                with pool.Fori(0, size) as i:
                    j, c = chunk_range(pool, b, start, i)
                    for t in range(2):
                        key_parts(c + 1, t)

                def shift_last(i):
                    pool.wait_ge(max_ok_a, b + 1)
                    at = kept(bounded(pool, i, 0, BLOCK - 1), 1, 1)
                    g.tensor_tensor(at, at, half(max_b, 1), ALU.subtract).then_inc(shifted_pool, 1)

                def context_parts(j, c, t):
                    pool.wait_ge(pv, c * 4 + (2 * t + 2))
                    g.tensor_copy(v_p[0][:, t, :], keys_n[:, bass.ds(j * 2 + t, 1), :].rearrange(
                        "p a d -> p (a d)")).then_inc(v_hi, 1)
                    pool.wait_ge(v_hi, c * 2 + (1 + t))
                    at = bounded(pool, j * 2 + t, 0, KT - 1)
                    g.tensor_tensor(v_p[1][:, t, :], keys_n[:, bass.ds(at, 1), :].rearrange(
                        "p a d -> p (a d)"), f(v_p[0][:, t, :]), ALU.subtract).then_inc(v_ok, 1)

                shift_last(0)
                with pool.Fori(0, size - 1) as i:
                    j, c = chunk_range(pool, b, start, i)
                    pool.wait_ge(keys_n_in, chunks * 16)
                    context_parts(j, c, 0)
                    shift_last(i + 1)
                    context_parts(j, c, 1)
                pool.wait_ge(keys_n_in, chunks * 16)
                j, c = chunk_range(pool, b, start, size - 1)
                for t in range(2):
                    context_parts(j, c, t)

            pool.wait_ge(norm_x, NT)
            pool.wait_ge(bvo_ok, 1)
            for i in range(NT):
                g.tensor_tensor(x_n[:, i, :], x_n[:, i, :], bo_row[:, :], ALU.add).then_inc(xb_ok, 1)
            pool.wait_ge(gate_in, 16)
            g.tensor_copy(gate_p[0][:, :], gate[:, :]).then_inc(gate_ok, 1)
            pool.wait_ge(gate_ok, 1)
            g.tensor_tensor(gate_p[1][:, :], gate[:, :], f(gate_p[0][:, :]), ALU.subtract).then_inc(gate_ok, 1)
            g.memset(earlier[:, :, :], 1.0).then_inc(pool_k, 1)
            g.memset(row_mask[:, :], 0.0).then_inc(pool_k, 1)
            pool.wait_ge(pool_k, 3)
            g.affine_select(out=earlier[:, :, :], in_=earlier[:, :, :], compare_op=ALU.is_gt, fill=0.0, base=0,
                            pattern=[[1, E], [-1, E]], channel_multiplier=0).then_inc(consts, 1)
            for n, base in enumerate((0, -E)):
                g.affine_select(out=row_mask[:, :], in_=row_mask[:, :], compare_op=ALU.not_equal, fill=1.0,
                                base=base, pattern=[[-1, E]], channel_multiplier=1).then_inc(consts, 1)
                pool.wait_ge(consts, 7 + n)

            pool.wait_ge(w_in, 32)
            g.tensor_copy(w_p[0][0][:, :], w_f[:, 0, :]).then_inc(first_w, 1)
            pool.wait_ge(first_w, 1)
            g.tensor_tensor(w_p[0][1][:, 0:4 * P], w_f[:, 0, 0:4 * P], f(w_p[0][0][:, 0:4 * P]),
                            ALU.subtract).then_inc(w_lo, 1)
            g.tensor_tensor(w_p[0][1][:, 4 * P:6 * P], w_f[:, 0, 4 * P:6 * P], f(w_p[0][0][:, 4 * P:6 * P]),
                            ALU.subtract).then_inc(wd_lo, 1)
            for h in range(2):
                pool.wait_ge(norm_var, h + 3)
                g.tensor_tensor(rstd[:, h * HT:(h + 1) * HT], var[:, h * HT:(h + 1) * HT],
                                neg_half[:, 0:HT], ALU.pow).then_inc(norm_rstd, 1)

            pool.sem_inc(inner_lo, 4)
            with pool.Fori(0, E // 2) as ep:
                for u in range(8):
                    n = ep * 8 + u
                    s = u % 4
                    pool.wait_ge(inner_hi, n + 1)
                    g.tensor_tensor(p_p[1][:, s, :], inner[:, s, :], f(p_p[0][:, s, :]),
                                    ALU.subtract).then_inc(inner_lo, 1)
                    if s == 3:
                        q = 1 - u // 4
                        pool.wait_ge(wd_hi, ep * 2 + (u // 4 + 1))
                        nxt = least(pool, ep * 2 + (1 + u // 4), E - 1, 1, E - 1)
                        g.tensor_tensor(w_p[q][1][:, 4 * P:6 * P],
                                        w_f[:, bass.ds(nxt, 1), 4 * P:6 * P].rearrange("p a d -> p (a d)"),
                                        f(w_p[q][0][:, 4 * P:6 * P]), ALU.subtract).then_inc(wd_lo, 1)

        @block.scalar
        def _(act):
            s = nc.scalar
            act.dma_start(wq, Wq).then_inc(wq_in, 16)
            for t, src in ((bq_c, bq), (bk_c, bk), (bv_c, bv)):
                act.dma_start(t[:, :], src).then_inc(col_in, 16)
            act.dma_start(bo_row[:, :], bo.to_broadcast([P, P])).then_inc(bo_in, 16)
            act.dma_start(wv_t[:, :], Wv_t).then_inc(wv_in, 16)
            act.dma_start(wo[:, :], Wo).then_inc(wv_in, 16)
            act.dma_start(gate[:, :], gate_t).then_inc(gate_in, 16)

            act.wait_ge(consts, 1)
            act.wait_ge(col_in, 48)
            s.activation(bv_mat, ones_f[:, :], ACT.Copy, scale=bv_c[:, :]).then_inc(bv_ok, 1)
            first, end, blocks, chunks = load_bounds(act)
            for h in range(2):
                act.wait_ge(tr_ps, h + 1)
                s.activation(half(xt_p[0], h), bank[4 + h][:, :], ACT.Copy).then_inc(xt_hi, 1)
            act.wait_ge(wvo_ps, 1)
            s.activation(wvo[:, :], bank[2][:, 0:P], ACT.Copy).then_inc(wvo_ok, 1)
            act.wait_ge(key_ps, 1)
            s.activation(k_s[:, :], bank[KEY_BANK][:, 0:CHUNK], ACT.Identity, bias=bk_c[:, :]).then_inc(key_kept, 1)
            for h in range(2):
                act.wait_ge(q_ps, h + 1)
                s.activation(half(q_p[0], h), bank[QUERY_BANK[h]][:, :], ACT.Identity,
                             bias=bq_c[:, :]).then_inc(q_hi, 1)
            act.wait_ge(key_cols, 1)
            act.sem_inc(score_kept, 4)
            act.sem_inc(alpha_ok, 2)

            with act.Fori(0, blocks) as b:
                start, size, done = block_range(act, first, end, b)
                with act.Fori(0, size) as i:
                    j, c = chunk_range(act, b, start, i)
                    for u, (t, h) in enumerate(UNITS):
                        if u == 1:
                            act.wait_ge(key_ps, c + 2)
                            act.wait_ge(k_lo, c * 2 + 2)
                            s.activation(k_s[:, :], bank[KEY_BANK][:, 0:CHUNK], ACT.Identity,
                                         bias=bk_c[:, :]).then_inc(key_kept, 1)
                        act.wait_ge(score_ps, c * 4 + (u + 5))
                        s.activation(kept(i, t, h), bank[SCORE_BANK[u]][:, :], ACT.Identity,
                                     bias=key_bias[:, bass.ds(j * 2 + t, 1)],
                                     scale=key_scale[:, bass.ds(j * 2 + t, 1)]).then_inc(score_kept, 1)
                act.wait_ge(max_cols, b * 2 + 1)
                for m in range(HT):
                    last = s.activation(max_mat[:, m, :], ident[:, :], ACT.Copy, scale=max_col[:, m:m + 1])
                last.then_inc(max_diag_a, 1)
                with act.If(b > 0):
                    for h in range(2):
                        act.wait_ge(old_diff, b * 2 + (h + 1))
                        s.activation(half(alpha, h), half(alpha, h), ACT.Exp).then_inc(alpha_ok, 1)
                act.wait_ge(old_diff, b * 2 + 2)
                act.wait_ge(max_ps, b * 2 + 2)
                s.activation(half(max_b, 1), bank[7][:, :], ACT.Copy).then_inc(max_ok_a, 1)
                with act.Fori(0, size) as i:
                    j, c = chunk_range(act, b, start, i)

                    def prob_high(u):
                        act.wait_ge(prob, c * 4 + (u + 1))
                        act.wait_ge(pv, c * 4 + (u + 1))
                        s.activation(p_p[0][:, u, :], bank[4 + u][:, :], ACT.Copy).then_inc(prob_hi, 1)

                    for u, (t, h) in enumerate(UNITS):
                        if u < 3:
                            act.wait_ge(shifted, c * 3 + (u + 1))
                        else:
                            act.wait_ge(prob_lo, c * 4 + (u + 1))
                            act.wait_ge(shifted_pool, c + 1)
                        s.activation(bank[4 + u][:, :], kept(i, t, h), ACT.Exp).then_inc(prob, 1)
                        if u > 0:
                            prob_high(u - 1)
                    prob_high(3)

            act.wait_ge(attn_end, 1)
            for h in range(2):
                s.activation(half(xt_p[0], h), bank[h][:, :], ACT.Copy).then_inc(o_hi, 1)
            for h in range(2):
                act.wait_ge(tr_ps, h + 3)
                s.activation(half(xt_p[0], h), bank[4 + h][:, :], ACT.Copy).then_inc(xt_hi, 1)
                act.wait_ge(x1_tr_ps, h + 1)
                s.activation(half(x1_t, h), bank[6 + h][:, :], ACT.Copy).then_inc(x1_t_ok, 1)
            act.wait_ge(logit_sub, 1)
            s.activation(r8[1], r8[0], ACT.Exp).then_inc(logit_exp, 1)

            s.activation(warm[:, :], neg_half[0:1, 0:1], ACT.Silu)

            act.wait_ge(comb_ps, 2)
            s.activation(half(comb_rows, 1), bank[3][0:2 * E, :], ACT.Copy).then_inc(comb_t_ok_a, 1)

            def weights_hi(ep, u, first_tile, end_tile, done):
                q = 1 - u // 4
                nxt = least(act, ep * 2 + (1 + u // 4), E - 1, 1, E - 1)
                s.activation(w_p[q][0][:, first_tile * P:end_tile * P],
                             w_f[:, bass.ds(nxt, 1), first_tile * P:end_tile * P].rearrange("p a d -> p (a d)"),
                             ACT.Copy).then_inc(done, 1)

            def inner_high(ep, u):
                n = ep * 8 + u
                act.wait_ge(inner_ok, n + 3)
                act.wait_ge(down, n + 1)
                s.activation(p_p[0][:, u % 4, :], inner[:, u % 4, :], ACT.Copy).then_inc(inner_hi, 1)

            with act.Fori(0, E // 2) as ep:
                for u in range(8):
                    n = ep * 8 + u
                    act.wait_ge(gate_ps, n + 1)
                    act.wait_ge(silc_ok, n + 1)
                    s.activation(silu[:, u % 2, :], bank[4 + 2 * (u % 2)][:, :], ACT.Silu).then_inc(silu_ok, 1)
                    if u > 0:
                        inner_high(ep, u - 1)
                    if u % 4 == 1:
                        act.wait_ge(up_ps, n)
                        weights_hi(ep, u, 0, 4, w_hi)
                    if u % 4 == 3:
                        act.wait_ge(down, ep * 8 + (u // 4 * 4 + 4))
                        weights_hi(ep, u, 4, 6, wd_hi)
                inner_high(ep, 7)

        @block.vector
        def _(dve):
            v = nc.vector
            chain = Chain(dve, dve_chain)
            for h in range(2):
                v.memset(half(run_max, h), LOWEST).then_inc(max_run, 1)
            dve.wait_ge(mask_in, 16)
            v.tensor_copy(mask_f[:, :], mask_u[:, :]).then_inc(mask_conv, 1)
            dve.wait_ge(mask_conv, 1)
            v.tensor_scalar(key_scale[:, :], mask_f[:, :], SCALE, None, ALU.mult).then_inc(mask_conv, 1)
            v.tensor_scalar(key_bias0[:, :], mask_f[:, :], 1.0, -MASKED,
                            ALU.subtract, ALU.mult).then_inc(mask_conv, 1)

            def norm_stats(src, i0, i1):
                for i in range(i0, i1):
                    chain.link(v.bn_stats(stats[:, i, :], src[:, i, :]))
                chain.settle()
                for i in range(i0, i1):
                    chain.link(v.bn_aggr(mv[:, i, :], stats[:, i, :]))
                chain.settle()
                v.tensor_scalar(var[:, i0:i1], mv[:, i0:i1, 1], EPS, None, ALU.add).then_inc(norm_var, 1)

            def norm_apply(src, i0, i1):
                for i in range(i0, i1):
                    v.tensor_scalar(xn[:, i, :], src[:, i, :], mv[:, i, 0:1], rstd[:, i:i + 1],
                                    ALU.subtract, ALU.mult).then_inc(norm_x, 1)

            dve.wait_ge(count_ps, 1)
            dve.wait_ge(consts, 4)
            chain.step(v.tensor_reduce(count[:, :], bank[6][0:1, 0:KT].rearrange("p (c t) -> p c t", t=2),
                                       X, ALU.add))
            chain.step(v.tensor_scalar(count[:, :], count[:, :], 0.0, None, ALU.is_gt))
            for i in range(2):
                chain.link(v.tensor_tensor(marked[:, i, :], count[:, :], chunk_no[:, i, :], ALU.mult))
            chain.settle()
            chain.step(v.tensor_reduce(edge[:, :], marked[:, :, :], X, ALU.max))
            chain.step(v.tensor_scalar(none[:, :], edge[:, :], 0.0, float(NC), ALU.is_equal, ALU.mult))
            chain.step(v.tensor_tensor(edge2[:, :], edge[:, :], none[:, :], ALU.add))
            chain.link(v.tensor_scalar(span[:, 0:1], edge2[:, 1:2], -1.0, float(NC), ALU.mult, ALU.add))
            chain.link(v.tensor_copy(span[:, 1:2], edge2[:, 0:1]))
            chain.settle()
            chain.step(v.tensor_tensor(span[:, 3:4], span[:, 1:2], span[:, 0:1], ALU.subtract))
            for i in range(3):
                chain.link(v.tensor_scalar(over[:, i:i + 1], span[:, 3:4], float(BLOCK * (i + 1)), None, ALU.is_gt))
            chain.settle()
            chain.step(v.tensor_reduce(span[:, 2:3], over[:, :], X, ALU.add))
            chain.step(v.tensor_scalar(span[:, 2:3], span[:, 2:3], 1.0, None, ALU.add))
            v.tensor_copy(bounds[:, :], span[:, :]).then_inc(bounds_ok, 1)

            dve.wait_ge(x_in, 16)
            for h in range(2):
                norm_stats(x_n, h * HT, (h + 1) * HT)
            for h in range(2):
                dve.wait_ge(norm_rstd, h + 1)
                norm_apply(x_n, h * HT, (h + 1) * HT)
            for h in range(2):
                dve.wait_ge(xt_hi, h + 1)
                v.tensor_tensor(half(xt_p[1], h), bank[4 + h][:, :], f(half(xt_p[0], h)),
                                ALU.subtract).then_inc(xt_lo, 1)
            dve.wait_ge(bo_in, 16)
            dve.wait_ge(bvo_ps, 1)
            v.tensor_tensor(bo_row[:, :], bo_row[:, :], bank[1][:, 0:P], ALU.add).then_inc(bvo_ok, 1)
            first, end, blocks, chunks = load_bounds(dve)
            for h in range(2):
                dve.wait_ge(q_hi, h + 1)
                v.scalar_tensor_tensor(half(q_p[1], h), bank[QUERY_BANK[h]][:, :], bq_c[:, :], f(half(q_p[0], h)),
                                       ALU.add, ALU.subtract).then_inc(q_lo, 1)

            dve.wait_ge(acc_zero, 1)
            dve.sem_inc(prob_lo, 4)
            dve.sem_inc(old_diff, 2)
            with dve.Fori(0, blocks) as b:
                start, size, done = block_range(dve, first, end, b)
                with dve.Fori(0, size) as i:
                    j, c = chunk_range(dve, b, start, i)
                    for u, (t, h) in enumerate(UNITS):
                        dve.wait_ge(score_kept, c * 4 + (u + 5))
                        dve.wait_ge(max_run, c * 4 + (u + 1))
                        v.tensor_tensor(half(run_max, h), half(run_max, h), kept(i, t, h),
                                        ALU.max).then_inc(max_run, 1)
                for h in range(2):
                    dve.wait_ge(max_tr, b * 2 + (h + 1))
                    v.tensor_reduce(max_col[:, h * HT:(h + 1) * HT],
                                    bank[4 + h][:, :].rearrange("p (i k) -> p i k", k=P), X, ALU.max)\
                        .then_inc(max_cols, 1)
                dve.wait_ge(max_cols, b * 2 + 2)
                for m in range(HT, NT):
                    last = v.tensor_scalar(max_mat[:, m, :], ident[:, :], max_col[:, m:m + 1], None, ALU.mult)
                last.then_inc(max_diag_v, 1)
                with dve.If(b > 0):
                    for h in range(2):
                        dve.wait_ge(max_ps, b * 2 + (h + 1))
                        v.tensor_tensor(half(alpha, h), half(max_b, h), bank[6 + h][:, :],
                                        ALU.subtract).then_inc(old_diff, 1)
                    for h in range(2):
                        dve.wait_ge(alpha_ok, b * 2 + (h + 1))
                        rows = slice(h * (P // 2), (h + 1) * (P // 2))
                        v.tensor_tensor(bank[h][:, :], bank[h][:, :], half(alpha, h), ALU.mult).then_inc(acc_zero, 1)
                        v.tensor_tensor(bank[2][rows, :], bank[2][rows, :], half(alpha, h)[rows, :],
                                        ALU.mult).then_inc(acc_zero, 1)

                def low(n, u):
                    dve.wait_ge(prob_hi, n)
                    v.tensor_tensor(p_p[1][:, u, :], bank[4 + u][:, :], f(p_p[0][:, u, :]),
                                    ALU.subtract).then_inc(prob_lo, 1)

                def shift(i, u):
                    t, h = UNITS[u]
                    at = kept(i, t, h)
                    v.tensor_tensor(at, at, half(max_b, h), ALU.subtract).then_inc(shifted, 1)

                dve.wait_ge(max_ps, b * 2 + 1)
                v.tensor_copy(half(max_b, 0), bank[6][:, :]).then_inc(max_ok, 1)
                for u in SHIFTS:
                    if u == 0:
                        dve.wait_ge(max_ok, b + 1)
                    if u == 1:
                        dve.wait_ge(max_ok_a, b + 1)
                    shift(0, u)
                with dve.Fori(0, size - 1) as i:
                    j, c = chunk_range(dve, b, start, i)
                    for u in range(4):
                        low(c * 4 + (u + 1), u)
                        if u < 3:
                            shift(i + 1, SHIFTS[u])
                j, c = chunk_range(dve, b, start, size - 1)
                for u in range(4):
                    low(c * 4 + (u + 1), u)

            dve.wait_ge(attn_end, 1)
            v.tensor_copy(sums, bank[2][:, :]).then_inc(row_ok, 1)
            for h in range(2):
                dve.wait_ge(o_hi, h + 1)
                v.tensor_tensor(half(xt_p[1], h), bank[h][:, :], f(half(xt_p[0], h)), ALU.subtract).then_inc(o_lo, 1)
            dve.wait_ge(sum_ps, 1)
            v.reciprocal(inv_sum[:, :].rearrange("p (h i) -> p h i", h=2),
                         bank[4][:, :].rearrange("p (i h k) -> p h i k", h=2, k=P // 2)[:, :, :, 0])\
                .then_inc(inv_ok, 1)
            dve.wait_ge(inv_ok, 1)
            for h in range(2):
                dve.wait_ge(attn_ps, h + 1)
                dve.wait_ge(xb_ok, (h + 1) * HT)
                for i in range(HT):
                    t = h * HT + i
                    v.scalar_tensor_tensor(x1[:, t, :], bank[6 + h][:, i * P:(i + 1) * P], inv_sum[:, t:t + 1],
                                           x_n[:, t, :], ALU.mult, ALU.add).then_inc(x1_ok, 1)
                dve.wait_ge(x1_ok, (h + 1) * HT)
                norm_stats(x1, h * HT, (h + 1) * HT)
            for h in range(2):
                dve.wait_ge(norm_rstd, h + 3)
                norm_apply(x1, h * HT, (h + 1) * HT)
            for h in range(2):
                dve.wait_ge(xt_hi, h + 3)
                v.tensor_tensor(half(xt_p[1], h), bank[4 + h][:, :], f(half(xt_p[0], h)),
                                ALU.subtract).then_inc(xt_lo, 1)

            dve.wait_ge(logit_ps, 1)
            logits = bank[2][:, 0:NT * E].rearrange("p (t e) -> p t e", e=E)
            chain.step(v.tensor_reduce(r1[0], logits, X, ALU.max))
            v.tensor_tensor(r8[0], logits, r1[0].unsqueeze(2).to_broadcast([P, NT, E]),
                            ALU.subtract).then_inc(logit_sub, 1)
            dve.wait_ge(logit_exp, 1)
            chain.step(v.tensor_reduce(r1[1], r8[1], X, ALU.add))
            chain.step(v.reciprocal(r1[2], r1[1]))
            chain.step(v.tensor_tensor(r8[2], r8[1], r1[2].unsqueeze(2).to_broadcast(
                [P, NT, E]), ALU.mult))
            chain.step(v.tensor_reduce(g4[0], r8[2].rearrange("p t (g k) -> p t g k", k=EG),
                                       X, ALU.max))

            def count_ahead(ahead, val, n):
                first_i = pair[0][:, :, 0:n, 0:n]
                second = pair[1][:, :, 0:n, 0:n]
                mine = val.unsqueeze(3).to_broadcast([P, NT, n, n])
                other = val.unsqueeze(2).to_broadcast([P, NT, n, n])
                chain.link(v.tensor_tensor(first_i, other, mine, ALU.is_equal))
                chain.link(v.tensor_tensor(second, other, mine, ALU.is_gt))
                chain.settle()
                chain.step(v.tensor_tensor(first_i, first_i, earlier[:, 0:n, 0:n].unsqueeze(1).to_broadcast(
                    [P, NT, n, n]), ALU.mult))
                chain.step(v.tensor_tensor(first_i, first_i, second, ALU.add))
                chain.step(v.tensor_reduce(ahead, first_i, X, ALU.add))

            count_ahead(g4[1], g4[0], G)
            by_group = [r.rearrange("p t (g k) -> p t g k", k=EG) for r in (r8[2], r8[3])]
            for k in range(EG):
                chain.link(v.scalar_tensor_tensor(by_group[1][:, :, :, k], g4[1], float(TOP),
                                                  by_group[0][:, :, :, k], ALU.is_lt, ALU.mult))
            chain.settle()
            count_ahead(r8[4], r8[3], E)
            chain.step(v.scalar_tensor_tensor(r8[5], r8[4], float(TOP), r8[3], ALU.is_lt, ALU.mult))
            chain.step(v.tensor_reduce(r1[0], r8[5], X, ALU.add))
            chain.step(v.reciprocal(r1[1], r1[0]))
            chain.step(v.tensor_tensor(r8[6], r8[5], r1[1].unsqueeze(2).to_broadcast(
                [P, NT, E]), ALU.mult))
            v.tensor_copy(comb[:, :, 0:E].bitcast(F32R), r8[6]).then_inc(comb_ok, 1)
            dve.wait_ge(comb_ok, 1)
            v.tensor_tensor(comb[:, :, E:2 * E], r8[6], comb[:, :, 0:E], ALU.subtract).then_inc(comb_ok, 1)
            v.tensor_scalar(pick[0][:, :], ones_f[0:2 * E, :], row_mask[:, 0:1], None, ALU.mult).then_inc(pick_ok, 1)
            dve.wait_ge(comb_ps, 1)
            v.tensor_copy(half(comb_rows, 0), bank[2][0:2 * E, :]).then_inc(comb_t_ok, 1)
            dve.sem_inc(silc_ok, 2)
            dve.sem_inc(inner_ok, 2)
            with dve.Fori(0, E // 2) as ep:
                for u in range(8):
                    n = ep * 8 + u
                    h = (u // 2) % 2
                    dve.wait_ge(silu_ok, n + 1)
                    dve.wait_ge(comb_b, ep * 4 + (u // 2 + 1))
                    v.tensor_tensor(silc[:, u % 2, :], silu[:, u % 2, :], bank[2 + h][:, :],
                                    ALU.mult).then_inc(silc_ok, 1)
                    dve.wait_ge(up_ps, n + 1)
                    dve.wait_ge(silc_ok, n + 3)
                    dve.wait_ge(inner_lo, n + 1)
                    v.tensor_tensor(inner[:, u % 4, :], silc[:, u % 2, :], bank[5 + 2 * (u % 2)][:, :],
                                    ALU.mult).then_inc(inner_ok, 1)
                    if u % 4 == 0:
                        q = 1 - u // 4
                        nxt = least(dve, ep * 2 + (1 + u // 4), E - 1, 1, E - 1)
                        v.tensor_scalar(pick[q][:, :], ones_f[0:2 * E, :], row_mask[:, bass.ds(nxt, 1)], None,
                                        ALU.mult).then_inc(pick_ok, 1)
                    if u % 4 == 2:
                        q = 1 - u // 4
                        nxt = least(dve, ep * 2 + (1 + u // 4), E - 1, 1, E - 1)
                        dve.wait_ge(w_hi, ep * 2 + (1 + u // 4))
                        v.tensor_tensor(w_p[q][1][:, 0:4 * P],
                                        w_f[:, bass.ds(nxt, 1), 0:4 * P].rearrange("p a d -> p (a d)"),
                                        f(w_p[q][0][:, 0:4 * P]), ALU.subtract).then_inc(w_lo, 1)
            dve.wait_ge(x1_t_ok, 2)
            for h in range(2):
                dve.wait_ge(y_end, h + 1)
                v.tensor_tensor(half(out_s, h), bank[h][:, :], half(x1_t, h), ALU.add).then_inc(out_ok, 1)

        @block.tensor
        def _(pe):
            mm = nc.tensor.matmul

            def product(out, lhs, rhs, start=True, stop=True):
                grouped = dict(skip_group_check=not (start and stop))
                mm(out, lhs[0], rhs[0], start=start, stop=False, **grouped)
                mm(out, lhs[1], rhs[0], start=False, stop=False, **grouped)
                return mm(out, lhs[0], rhs[1], start=False, stop=stop, **grouped)

            def halves(t, h):
                return tuple(half(x_, h) for x_ in t)

            def keep_clock(products, banks, start=False):
                for n in range(products):
                    mm(bank[banks[n % len(banks)]][:, :], zeros_b[:, :], zeros_b[:, 0:1].to_broadcast([P, HALF]),
                       start=start and n < len(banks), stop=False, skip_group_check=True)

            pe.wait_ge(consts, 1)
            pe.wait_ge(mask_conv, 1)
            mm(bank[6][0:1, 0:KT], ones_f[:, 0:1], mask_f[:, :], start=True, stop=True).then_inc(count_ps, 1)
            pe.wait_ge(zero_ok, 1)
            first, end, blocks, chunks = load_bounds(pe)
            pe.wait_ge(wv_in, 32)
            mm(bank[2][:, 0:P], wv_t[:, :], wo[:, :], start=True, stop=True).then_inc(wvo_ps, 1)
            pe.wait_ge(bv_ok, 1)
            mm(bank[1][:, 0:P], bv_mat, wo[:, :], start=True, stop=True).then_inc(bvo_ps, 1)
            pe.wait_ge(consts, 2)
            for h in range(2):
                for i in range(HT):
                    pe.wait_ge(norm_x, h * HT + i + 1)
                    last = nc.tensor.transpose(bank[4 + h][:, i * P:(i + 1) * P], xn[:, h * HT + i, :], ident[:, :])
                last.then_inc(tr_ps, 1)
            pe.sem_inc(score_ps, 4)
            pe.wait_ge(wk_in, 16)
            pe.wait_ge(first_keys_in, 16)
            mm(bank[KEY_BANK][:, 0:CHUNK], wk[:, :], keys_t[:, bass.ds(first * CHUNK, CHUNK)],
               start=True, stop=True).then_inc(key_ps, 1)
            pe.wait_ge(pool_w, 2)
            for h in range(2):
                pe.wait_ge(xt_lo, h + 1)
                product(bank[QUERY_BANK[h]][:, :], [w[:, :] for w in wq_p], halves(xt_p, h)).then_inc(q_ps, 1)

            pe.wait_ge(ones_ok, 4)
            pe.wait_ge(wvo_ok, 1)
            pe.wait_ge(bvo_ok, 1)
            pe.sem_inc(keys_t_in, 16)
            pe.wait_ge(keys_t_in, chunks * 16)
            for n in range(3):
                last = mm(bank[n][:, :], zeros_b[:, :], zeros_b[:, 0:1].to_broadcast([P, HALF]), start=True,
                          stop=False, skip_group_check=True)
            last.then_inc(acc_zero, 1)
            pe.sem_inc(pv, 4)
            with pe.Fori(0, blocks) as b:
                start, size, done = block_range(pe, first, end, b)
                with pe.Fori(0, size) as i:
                    j, c = chunk_range(pe, b, start, i)
                    for u, (t, h) in enumerate(UNITS):
                        if u == 0:
                            pe.wait_ge(q_lo, 2)
                        if h == 0:
                            pe.wait_ge(k_lo, c * 2 + (t + 1))
                        if u == 1:
                            nxt = least(pe, j + 1, end - 1, 0, NC - 1)
                            mm(bank[KEY_BANK][:, 0:CHUNK], wk[:, :], keys_t[:, bass.ds(nxt * CHUNK, CHUNK)],
                               start=True, stop=True).then_inc(key_ps, 1)
                        pe.wait_ge(score_kept, c * 4 + (u + 1))
                        product(bank[SCORE_BANK[u]][:, :], [k[:, t, :] for k in k_p],
                                halves(q_p, h)).then_inc(score_ps, 1)
                for h in range(2):
                    pe.wait_ge(max_run, done * 4 + (h + 1))
                    for i in range(HT):
                        last = nc.tensor.transpose(bank[4 + h][:, i * P:(i + 1) * P],
                                                   tile(run_max, h * HT + i), ident[:, :])
                    last.then_inc(max_tr, 1)
                keep_clock(FILL_MAXIMA, (0, 1, 2))
                for h in range(2):
                    pe.wait_ge(max_diag_v if h else max_diag_a, b + 1)
                    for i in range(HT):
                        last = mm(bank[6 + h][:, i * P:(i + 1) * P], ones_f[:, :], max_mat[:, h * HT + i, :],
                                  start=True, stop=True)
                    last.then_inc(max_ps, 1)
                pe.wait_ge(acc_zero, b * 4 + 1)
                keep_clock(FILL_SHIFT, (0, 1, 2))
                with pe.Fori(0, size) as i:
                    j, c = chunk_range(pe, b, start, i)
                    for u, (t, h) in enumerate(UNITS):
                        if h == 0:
                            pe.wait_ge(v_ok, c * 2 + (t + 1))
                        pe.wait_ge(prob_lo, c * 4 + (u + 5))
                        product(bank[h][:, :], [w[:, t, :] for w in v_p], [w[:, u, :] for w in p_p],
                                start=False, stop=False)
                        for w in p_p:
                            last = mm(bank[2][:, :], ones_half[h][:, :], w[:, u, :], start=False, stop=False,
                                      skip_group_check=True)
                        last.then_inc(pv, 1)
            for n in range(3):
                last = mm(bank[n][:, :], zeros_b[:, :], zeros_b[:, 0:1].to_broadcast([P, HALF]), start=False,
                          stop=True, skip_group_check=True)
            last.then_inc(attn_end, 1)

            keep_clock(FILL_VALUES, (5,), start=True)
            pe.wait_ge(pool_w, 4)
            pe.wait_ge(row_ok, 1)
            for i in range(HT):
                last = nc.tensor.transpose(bank[4][:, i * P:(i + 1) * P], tile(sums, i), ident[:, :])
            last.then_inc(sum_ps, 1)
            for h in range(2):
                pe.wait_ge(o_lo, h + 1)
                for i in range(HT):
                    last = product(bank[6 + h][:, i * P:(i + 1) * P], [tile(w, h * HT + i) for w in xt_p],
                                   [w[:, :] for w in wvo_p])
                last.then_inc(attn_ps, 1)
            keep_clock(FILL_NORM, (0, 1), start=True)
            for h in range(2):
                for i in range(HT):
                    pe.wait_ge(norm_x, NT + h * HT + i + 1)
                    last = nc.tensor.transpose(bank[4 + h][:, i * P:(i + 1) * P], xn[:, h * HT + i, :], ident[:, :])
                last.then_inc(tr_ps, 1)
                for i in range(HT):
                    last = nc.tensor.transpose(bank[6 + h][:, i * P:(i + 1) * P], x1[:, h * HT + i, :], ident[:, :])
                last.then_inc(x1_tr_ps, 1)
            pe.wait_ge(gate_ok, 2)
            for i in range(NT):
                if i % HT == 0:
                    pe.wait_ge(xt_lo, 3 + i // HT)
                last = product(bank[2][:, i * E:(i + 1) * E], [tile(w, i) for w in xt_p], [w[:, :] for w in gate_p])
            last.then_inc(logit_ps, 1)

            def gate_up(u):
                h, it, q = (u // 2) % 2, u % 2, u // 4
                product(bank[4 + 2 * (u % 2)][:, :], [tile(w, it) for w in w_p[q]],
                        halves(xt_p, h)).then_inc(gate_ps, 1)
                product(bank[5 + 2 * (u % 2)][:, :], [tile(w, 2 + it) for w in w_p[q]],
                        halves(xt_p, h)).then_inc(up_ps, 1)

            def down_product(u, low_parts):
                h, it, q = (u // 2) % 2, u % 2, u // 4
                pe.wait_ge(inner_lo, low_parts)
                product(bank[h][:, :], [tile(w, 4 + it) for w in w_p[q]], [w[:, u % 4, :] for w in p_p],
                        start=False, stop=False).then_inc(down, 1)

            def combine(q, h, n):
                pe.wait_ge(pick_ok, n)
                mm(bank[2 + h][:, :], pick[q][:, :], half(comb_rows, h), start=True,
                   stop=True).then_inc(comb_b, 1)

            pe.wait_ge(x1_t_ok, 2)
            pe.wait_ge(w_lo, 1)
            for u in range(2):
                gate_up(u)
            keep_clock(FILL_ROUTING, (0, 1))
            pe.wait_ge(comb_ok, 2)
            for h in range(2):
                for i in range(HT):
                    last = nc.tensor.transpose(bank[2 + h][0:2 * E, i * P:(i + 1) * P], comb[:, h * HT + i, :],
                                               ident[:, :])
                last.then_inc(comb_ps, 1)
            keep_clock(FILL_COMBINE, (0, 1))
            for h in range(2):
                pe.wait_ge(comb_t_ok_a if h else comb_t_ok, 1)
                combine(0, h, 1)

            def gate_up_ahead(ep, u):
                n = ep * 8 + u
                m = (u + 2) % 8
                if m % 4 == 0:
                    pe.wait_ge(w_lo, ep * 2 + ((u + 2) // 4 + 1))
                pe.wait_ge(inner_ok, n + 3)
                gate_up(m)
                if m % 2 == 0:
                    pe.wait_ge(silc_ok, n + 4)
                    combine(((u + 4) // 4) % 2, 1 - (m // 2) % 2, ep * 2 + (1 + (u + 4) // 4))

            pe.sem_inc(down, 4)
            with pe.Fori(0, E // 2) as ep:
                for u in range(8):
                    if u < 6:
                        gate_up_ahead(ep, u)
                    else:
                        with pe.If(ep < E // 2 - 1):
                            gate_up_ahead(ep, u)
                    if u > 0:
                        if u % 4 == 1:
                            pe.wait_ge(wd_lo, ep * 2 + (u // 4 + 1))
                        down_product(u - 1, ep * 8 + (u + 4))
                    else:
                        with pe.If(ep > 0):
                            down_product(7, ep * 8 + 4)
            for h in range(2):
                if h == 1:
                    down_product(7, E * 4 + 4)
                mm(bank[h][:, :], zeros_b[:, :], zeros_b[:, 0:1].to_broadcast([P, HALF]), start=False, stop=True,
                   skip_group_check=True).then_inc(y_end, 1)


_INS = ["x", "mask", "ctx_t", "ctx_n", "Wq", "bq", "Wk", "bk", "Wv_t", "bv", "Wo", "bo", "gate_t", "w13_t", "w2_t"]


def kernel(**inputs):
    import numpy as np
    import concourse.bacc as bacc
    from concourse.bass_utils import run_bass_kernel_spmd

    a = {k.replace("L0_xattn_", "").replace("L0_ffn_", ""): np.asarray(v) for k, v in inputs.items()}
    context = a["ctx_1024"][0]
    keys, width = context.shape
    whole = -(-keys // CHUNK) * CHUNK
    padded = np.zeros((whole, width), context.dtype)
    padded[whole - keys:] = context
    mask = np.zeros(whole, np.uint8)
    mask[whole - keys:] = a["mask_BxS2_bk0"][0].view(np.uint8)
    experts, _, inter = a["w2_weight"].shape
    data = {
        "x": a["x"][0],
        "mask": np.ascontiguousarray(mask.reshape(-1, P).T).view(np.uint32),
        "ctx_t": padded.T,
        "ctx_n": padded.reshape(-1, P, width).transpose(1, 0, 2),
        "Wv_t": a["Wv"].T,
        "gate_t": a["gate_w"].T,
        "w13_t": a["w13_weight"].transpose(2, 0, 1),
        "w2_t": a["w2_weight"].reshape(experts, width, inter // P, P).transpose(3, 0, 2, 1).reshape(P, experts, -1),
    }
    for name in ("Wq", "Wk", "Wo"):
        data[name] = a[name]
    for name in ("bq", "bk", "bv"):
        data[name] = a[name].reshape(P, 1)
    data["bo"] = a["bo"].reshape(1, P)

    nc = bacc.Bacc("TRN2", target_bir_lowering=False, num_devices=1)
    arrays, args = {}, []
    for name in _INS:
        array = np.ascontiguousarray(data[name])
        arrays[f"in_{name}"] = array
        args.append(nc.dram_tensor(f"in_{name}", array.shape, mybir.dt.from_np(array.dtype),
                                   kind="ExternalInput").ap())
    tokens = data["x"].shape[0]
    out = nc.dram_tensor("out_t", (width, tokens), F32, kind="ExternalOutput").ap()
    xattn_ffn(nc, keys, *args, out)
    result = run_bass_kernel_spmd(nc, [arrays], core_ids=[0])
    return np.ascontiguousarray(result.results[0]["out_t"].T).reshape(1, tokens, width)
```
